# Optimizing a Trainium2 kernel written in Bass

```python
import numpy as np
import jax
import jax.numpy as jnp

def _softmax(x, axis=-1):
    return jax.nn.softmax(x, axis=axis)

def _gelu(x):
    return jax.nn.gelu(x, approximate=True)

def _silu(x):
    return jax.nn.silu(x)

def _sigmoid(x):
    return jax.nn.sigmoid(x)

def _layernorm(x, axis=-1, eps=1e-05):
    m = jnp.mean(x, axis=axis, keepdims=True)
    v = jnp.var(x, axis=axis, keepdims=True)
    return (x - m) / jnp.sqrt(v + eps)

def _scatter_add(tgt, idx, src, axis=0):
    return tgt.at[idx].add(src)

def _segment_sum(src, seg, n):
    return jax.ops.segment_sum(src, seg, n)
kernel_name = 'mk_early_fusion_embed_d1_tok_img2048_r4_a52673'

def setup_inputs(seed: int=0):
    np.random.seed(seed)
    _w = jnp.asarray

    def _rec_inputs():
        import jax
        import jax.numpy as jnp
        _rk = jax.random.key(seed)
        x = -0.0043416 + 0.998921 * jax.random.normal(jax.random.fold_in(_rk, 1), (16, 64, 64, 2), jnp.float32)
        x_txt = jax.random.randint(jax.random.fold_in(_rk, 51), (16, 128), 0, 168, jnp.int32)
        return (x, x_txt)
    x, x_txt = _rec_inputs()

    def _L0_tok_setup():
        import jax, jax.numpy as jnp
        import numpy as np
        H, N, CH = (64, 64, 1)

        def _r2c(x):
            return x[..., 0] + 1j * x[..., 1]

        def _bilinear(dt, Ac, Bc):
            n = Ac.shape[-1]
            I = jnp.eye(n, dtype=Ac.dtype)
            half = (dt.astype(Ac.real.dtype) / 2)[:, None]
            A_back = I - half * Ac
            A_fwd = I + half * Ac
            dB = dt.astype(Ac.dtype) * jnp.linalg.solve(A_back, Bc[..., None])[..., 0]
            dA = jnp.linalg.solve(A_back, A_fwd)
            return (dA, dB)

        def _krylov(L, dA, dB):
            x = dB[..., None]
            A_ = dA
            while x.shape[-1] < L:
                x = jnp.concatenate([x, jnp.einsum('hnm,hml->hnl', A_, x)], axis=-1)
                A_ = A_ @ A_
            return x[..., :L]
        key = jax.random.key(seed)
        kA, kB, kC, kdt = jax.random.split(key, 4)
        M = jax.random.normal(kA, (H, N, N, 2), dtype=jnp.float32) / np.float32(np.sqrt(N))
        Mc = _r2c(M)
        Ac = 0.5 * (Mc - jnp.conjugate(jnp.swapaxes(Mc, -1, -2))) - 0.5 * jnp.eye(N, dtype=Mc.dtype)
        A = jnp.stack([Ac.real, Ac.imag], axis=-1)
        B = jax.random.normal(kB, (H, N, 2), dtype=jnp.float32)
        C = jax.random.normal(kC, (CH, H, N, 2), dtype=jnp.float32)
        log_dt = jax.random.uniform(kdt, (H, 1), dtype=jnp.float32, minval=np.float32(np.log(0.001)), maxval=np.float32(np.log(0.1)))
        return {'A': A, 'B': B, 'C': C, 'log_dt': log_dt, 'L': 512}
    _L0_tok_all = _L0_tok_setup()
    _L0_tok_in = {k: v for k, v in _L0_tok_all.items() if k in ('A', 'B', 'log_dt')}
    del _L0_tok_all

    def _L0_txt_setup():
        import jax, jax.numpy as jnp
        import numpy as np
        NUM_SLOTS = 168
        NUM_CATS = 512
        BATCH, SEQ = (128, 200)
        key = jax.random.key(seed)
        k1, k2 = jax.random.split(key)
        inputs_hour = jax.random.randint(k1, (BATCH, SEQ), 0, NUM_SLOTS)
        catid_time_matrix = jax.random.normal(k2, (NUM_SLOTS, NUM_CATS), dtype=jnp.float32)
        return {'inputs_hour': inputs_hour, 'catid_time_matrix': catid_time_matrix}
    _L0_txt_all = _L0_txt_setup()
    _L0_txt_in = {k: v for k, v in _L0_txt_all.items() if k in ('catid_time_matrix',)}
    del _L0_txt_all

    def _L0_attn_setup():
        import jax, jax.numpy as jnp
        import numpy as np
        D_MODEL = 512
        EXPAND = 2
        HEADDIM = 64
        D_STATE = 64
        D_CONV = 4
        D_INNER = EXPAND * D_MODEL
        NHEADS = D_INNER // HEADDIM
        NGROUPS = 1
        CONV_DIM = D_INNER + 2 * NGROUPS * D_STATE
        D_IN_PROJ = 2 * D_INNER + 2 * NGROUPS * D_STATE + NHEADS
        BATCH = 1
        SEQLEN = 256
        RMS_EPS = 1e-05
        key = jax.random.key(seed)
        ks = jax.random.split(key, 8)
        x = jax.random.normal(ks[0], (BATCH, SEQLEN, D_MODEL), jnp.float32)
        W_in = jax.random.normal(ks[1], (D_IN_PROJ, D_MODEL), jnp.float32) * 0.02
        conv_w = jax.random.normal(ks[2], (CONV_DIM, D_CONV), jnp.float32) * 0.2
        conv_b = jnp.zeros((CONV_DIM,), jnp.float32)
        dt_bias = jax.random.uniform(ks[3], (NHEADS,), jnp.float32, -6.0, -3.0)
        A_log = jnp.log(1.0 + 15.0 * jax.random.uniform(ks[4], (NHEADS,), jnp.float32))
        D = jnp.ones((NHEADS,), jnp.float32)
        norm_w = jnp.ones((D_INNER,), jnp.float32)
        W_out = jax.random.normal(ks[5], (D_MODEL, D_INNER), jnp.float32) * 0.02
        return {'x': x, 'W_in': W_in, 'conv_w': conv_w, 'conv_b': conv_b, 'dt_bias': dt_bias, 'A_log': A_log, 'D': D, 'norm_w': norm_w, 'W_out': W_out}
    _L0_attn_all = _L0_attn_setup()
    _L0_attn_in = {k: v for k, v in _L0_attn_all.items() if k in ('W_in', 'conv_w', 'conv_b', 'dt_bias', 'A_log', 'D', 'norm_w', 'W_out')}
    del _L0_attn_all

    def _L0_ffn_setup():
        import jax, jax.numpy as jnp
        import numpy as np
        NUM_EXPERTS = 32
        TOP_K = 8
        SELECT_TOP_K = 4
        THRESHOLD = 0.5
        HIDDEN = 512
        D_FF = 192

        def _moe_forward(hidden_states, gate_weight, gate_up_proj, down_proj, similarity):
            B, S_len, H = hidden_states.shape
            E, K, Ssel = (NUM_EXPERTS, TOP_K, SELECT_TOP_K)
            x = hidden_states.reshape(-1, H)
            router_logits = x @ gate_weight.T
            router_probs = jax.nn.softmax(router_logits.astype(jnp.float32), axis=-1).astype(router_logits.dtype)
            router_top_value, router_indices = jax.lax.top_k(router_probs, K)
            routing_weights = router_top_value / jnp.clip(jnp.sum(router_top_value, axis=-1, keepdims=True), 1e-12, None)
            sim = similarity.astype(jnp.float32)
            sim = sim.at[jnp.arange(E), jnp.arange(E)].set(1.0)
            prim = router_indices[:, :Ssel]
            sec = router_indices[:, Ssel:]
            sim_cand = sim[sec[:, :, None], prim[:, None, :]]
            best_sim = jnp.max(sim_cand, axis=-1)
            best_i = jnp.argmax(sim_cand, axis=-1)
            prim_rep = jnp.broadcast_to(prim[:, None, :], sim_cand.shape)
            best_primary = jnp.take_along_axis(prim_rep, best_i[..., None], axis=-1)[..., 0]
            new_sec = jnp.where(best_sim < THRESHOLD, sec, best_primary) if THRESHOLD > 0.0 else best_primary
            rerouted_indices = jnp.concatenate([prim, new_sec], axis=1)
            combine = jnp.sum(jax.nn.one_hot(rerouted_indices, E, dtype=routing_weights.dtype) * routing_weights[..., None], axis=1)

            def expert_step(y, params):
                wgu, wd, cw = params
                gu = x @ wgu.T
                g, u = jnp.split(gu, 2, axis=-1)
                h = jax.nn.silu(g) * u
                y = y + h @ wd.T * cw[:, None]
                return (y, None)
            y0 = jnp.zeros_like(x)
            y, _ = jax.lax.scan(expert_step, y0, (gate_up_proj, down_proj, combine.T))
            return y.reshape(B, S_len, H)
        key = jax.random.key(seed)
        ks = jax.random.split(key, 5)
        hidden_states = jax.random.normal(ks[0], (4, 512, HIDDEN), dtype=jnp.float32)
        gate_weight = jax.random.normal(ks[1], (NUM_EXPERTS, HIDDEN), dtype=jnp.float32) * 0.02
        gate_up_proj = jax.random.normal(ks[2], (NUM_EXPERTS, 2 * D_FF, HIDDEN), dtype=jnp.float32) * 0.02
        down_proj = jax.random.normal(ks[3], (NUM_EXPERTS, HIDDEN, D_FF), dtype=jnp.float32) * 0.02
        similarity = jax.random.uniform(ks[4], (NUM_EXPERTS, NUM_EXPERTS), dtype=jnp.float32)
        return {'hidden_states': hidden_states, 'gate_weight': gate_weight, 'gate_up_proj': gate_up_proj, 'down_proj': down_proj, 'similarity': similarity}
    _L0_ffn_all = _L0_ffn_setup()
    _L0_ffn_in = {k: v for k, v in _L0_ffn_all.items() if k in ('gate_weight', 'gate_up_proj', 'down_proj', 'similarity')}
    del _L0_ffn_all
    return {'x': x, 'x_txt': x_txt, 'L0_tok_A': _L0_tok_in['A'], 'L0_tok_B': _L0_tok_in['B'], 'L0_tok_log_dt': _L0_tok_in['log_dt'], 'L0_txt_catid_time_matrix': _L0_txt_in['catid_time_matrix'], 'L0_attn_W_in': _L0_attn_in['W_in'], 'L0_attn_conv_w': _L0_attn_in['conv_w'], 'L0_attn_conv_b': _L0_attn_in['conv_b'], 'L0_attn_dt_bias': _L0_attn_in['dt_bias'], 'L0_attn_A_log': _L0_attn_in['A_log'], 'L0_attn_D': _L0_attn_in['D'], 'L0_attn_norm_w': _L0_attn_in['norm_w'], 'L0_attn_W_out': _L0_attn_in['W_out'], 'L0_ffn_gate_weight': _L0_ffn_in['gate_weight'], 'L0_ffn_gate_up_proj': _L0_ffn_in['gate_up_proj'], 'L0_ffn_down_proj': _L0_ffn_in['down_proj'], 'L0_ffn_similarity': _L0_ffn_in['similarity']}

def reference(x, x_txt, L0_tok_A, L0_tok_B, L0_tok_log_dt, L0_txt_catid_time_matrix, L0_attn_W_in, L0_attn_conv_w, L0_attn_conv_b, L0_attn_dt_bias, L0_attn_A_log, L0_attn_D, L0_attn_norm_w, L0_attn_W_out, L0_ffn_gate_weight, L0_ffn_gate_up_proj, L0_ffn_down_proj, L0_ffn_similarity):
    import jax
    import jax.numpy as jnp

    def _L0_tok_ref(A, B, C, log_dt, L):
        import jax, jax.numpy as jnp
        import numpy as np
        H, N, CH = (64, 64, 1)

        def _r2c(x):
            return x[..., 0] + 1j * x[..., 1]

        def _bilinear(dt, Ac, Bc):
            n = Ac.shape[-1]
            I = jnp.eye(n, dtype=Ac.dtype)
            half = (dt.astype(Ac.real.dtype) / 2)[:, None]
            A_back = I - half * Ac
            A_fwd = I + half * Ac
            dB = dt.astype(Ac.dtype) * jnp.linalg.solve(A_back, Bc[..., None])[..., 0]
            dA = jnp.linalg.solve(A_back, A_fwd)
            return (dA, dB)

        def _krylov(L, dA, dB):
            x = dB[..., None]
            A_ = dA
            while x.shape[-1] < L:
                x = jnp.concatenate([x, jnp.einsum('hnm,hml->hnl', A_, x)], axis=-1)
                A_ = A_ @ A_
            return x[..., :L]
        Ac, Bc, Cc = (_r2c(A), _r2c(B), _r2c(C))
        dt = jnp.exp(log_dt)
        dA, dB = _bilinear(dt, Ac, Bc)
        x = _krylov(L, dA, dB)
        k = jnp.einsum('chn,hnl->chl', Cc, x).real.astype(jnp.float32)
        return k

    def _L0_txt_ref(inputs_hour, catid_time_matrix):
        import jax, jax.numpy as jnp
        import numpy as np
        NUM_SLOTS = 168
        NUM_CATS = 512
        BATCH, SEQ = (128, 200)
        probs = jax.nn.softmax(catid_time_matrix, axis=1)
        return probs[inputs_hour]

    def _L0_attn_ref(x, W_in, conv_w, conv_b, dt_bias, A_log, D, norm_w, W_out):
        import jax, jax.numpy as jnp
        import numpy as np
        D_MODEL = 512
        EXPAND = 2
        HEADDIM = 64
        D_STATE = 64
        D_CONV = 4
        D_INNER = EXPAND * D_MODEL
        NHEADS = D_INNER // HEADDIM
        NGROUPS = 1
        CONV_DIM = D_INNER + 2 * NGROUPS * D_STATE
        D_IN_PROJ = 2 * D_INNER + 2 * NGROUPS * D_STATE + NHEADS
        BATCH = 1
        SEQLEN = 256
        RMS_EPS = 1e-05
        B, T, _ = x.shape
        zxbcdt = jnp.einsum('btd,pd->btp', x, W_in)
        z = zxbcdt[..., :D_INNER]
        xBC = zxbcdt[..., D_INNER:D_INNER + CONV_DIM]
        dt = jax.nn.softplus(zxbcdt[..., D_INNER + CONV_DIM:] + dt_bias)
        xp = jnp.pad(xBC, ((0, 0), (D_CONV - 1, 0), (0, 0)))
        conv = conv_b + sum((xp[:, k:k + T, :] * conv_w[:, k] for k in range(D_CONV)))
        xBC = jax.nn.silu(conv)
        xh = xBC[..., :D_INNER].reshape(B, T, NHEADS, HEADDIM)
        Bm = xBC[..., D_INNER:D_INNER + D_STATE]
        Cm = xBC[..., D_INNER + D_STATE:]
        A = -jnp.exp(A_log)
        dA = jnp.exp(dt * A)

        def step(h, inp):
            dA_t, dt_t, B_t, x_t, C_t = inp
            h = h * dA_t[:, :, None, None] + jnp.einsum('bh,bn,bhp->bhpn', dt_t, B_t, x_t)
            y_t = jnp.einsum('bhpn,bn->bhp', h, C_t)
            return (h, y_t)
        h0 = jnp.zeros((B, NHEADS, HEADDIM, D_STATE), x.dtype)
        xs = (dA.transpose(1, 0, 2), dt.transpose(1, 0, 2), Bm.transpose(1, 0, 2), xh.transpose(1, 0, 2, 3), Cm.transpose(1, 0, 2))
        _, ys = jax.lax.scan(step, h0, xs)
        y = ys.transpose(1, 0, 2, 3) + D[None, None, :, None] * xh
        y = y.reshape(B, T, D_INNER)
        y = y * jax.nn.silu(z)
        y = y * jax.lax.rsqrt(jnp.mean(y * y, axis=-1, keepdims=True) + RMS_EPS) * norm_w
        return jnp.einsum('bti,di->btd', y, W_out)

    def _L0_ffn_ref(hidden_states, gate_weight, gate_up_proj, down_proj, similarity):
        import jax, jax.numpy as jnp
        import numpy as np
        NUM_EXPERTS = 32
        TOP_K = 8
        SELECT_TOP_K = 4
        THRESHOLD = 0.5
        HIDDEN = 512
        D_FF = 192

        def _moe_forward(hidden_states, gate_weight, gate_up_proj, down_proj, similarity):
            B, S_len, H = hidden_states.shape
            E, K, Ssel = (NUM_EXPERTS, TOP_K, SELECT_TOP_K)
            x = hidden_states.reshape(-1, H)
            router_logits = x @ gate_weight.T
            router_probs = jax.nn.softmax(router_logits.astype(jnp.float32), axis=-1).astype(router_logits.dtype)
            router_top_value, router_indices = jax.lax.top_k(router_probs, K)
            routing_weights = router_top_value / jnp.clip(jnp.sum(router_top_value, axis=-1, keepdims=True), 1e-12, None)
            sim = similarity.astype(jnp.float32)
            sim = sim.at[jnp.arange(E), jnp.arange(E)].set(1.0)
            prim = router_indices[:, :Ssel]
            sec = router_indices[:, Ssel:]
            sim_cand = sim[sec[:, :, None], prim[:, None, :]]
            best_sim = jnp.max(sim_cand, axis=-1)
            best_i = jnp.argmax(sim_cand, axis=-1)
            prim_rep = jnp.broadcast_to(prim[:, None, :], sim_cand.shape)
            best_primary = jnp.take_along_axis(prim_rep, best_i[..., None], axis=-1)[..., 0]
            new_sec = jnp.where(best_sim < THRESHOLD, sec, best_primary) if THRESHOLD > 0.0 else best_primary
            rerouted_indices = jnp.concatenate([prim, new_sec], axis=1)
            combine = jnp.sum(jax.nn.one_hot(rerouted_indices, E, dtype=routing_weights.dtype) * routing_weights[..., None], axis=1)

            def expert_step(y, params):
                wgu, wd, cw = params
                gu = x @ wgu.T
                g, u = jnp.split(gu, 2, axis=-1)
                h = jax.nn.silu(g) * u
                y = y + h @ wd.T * cw[:, None]
                return (y, None)
            y0 = jnp.zeros_like(x)
            y, _ = jax.lax.scan(expert_step, y0, (gate_up_proj, down_proj, combine.T))
            return y.reshape(B, S_len, H)
        return _moe_forward(hidden_states, gate_weight, gate_up_proj, down_proj, similarity)
    h = _L0_tok_ref(L0_tok_A, L0_tok_B, x, L0_tok_log_dt, 512)
    h = jnp.concatenate([h, _L0_txt_ref(x_txt, L0_txt_catid_time_matrix)], axis=1)
    h = h + _L0_attn_ref(_layernorm(h, axis=-1), L0_attn_W_in, L0_attn_conv_w, L0_attn_conv_b, L0_attn_dt_bias, L0_attn_A_log, L0_attn_D, L0_attn_norm_w, L0_attn_W_out)
    h = h + _L0_ffn_ref(_layernorm(h, axis=-1), L0_ffn_gate_weight, L0_ffn_gate_up_proj, L0_ffn_down_proj, L0_ffn_similarity)
    return h

_drawn_inputs = setup_inputs


def setup_inputs(seed=0):
    import zlib

    import numpy as np

    out = dict(_drawn_inputs(seed))
    spreads = {'L0_attn_conv_b': (0.0, 0.1), 'L0_attn_D': (1.0, 0.2), 'L0_attn_norm_w': (1.0, 0.2)}
    factors = {}
    for name, (base, spread) in spreads.items():
        noise = np.random.default_rng([zlib.crc32(name.encode()), seed]).standard_normal(out[name].shape)
        drawn = base * np.exp(spread * noise) if base else spread * noise
        out[name] = jnp.asarray(drawn.astype(out[name].dtype))
    for name, factor in factors.items():
        out[name] = (out[name] * factor).astype(out[name].dtype)
    return out
```

```python
import concourse.bass as bass
from concourse import mybir
from contextlib import ExitStack

FP32 = mybir.dt.float32
BF16 = mybir.dt.bfloat16
I32 = mybir.dt.int32
U32 = mybir.dt.uint32
ALU = mybir.AluOpType
ACT = mybir.ActivationFunctionType
AX = mybir.AxisListType
P = 128


class Scope:

    def __init__(self, nc, ctx, tag):
        self.nc, self.ctx, self.tag = nc, ctx, tag

    def sb(self, name, shape, dt=FP32):
        return self.ctx.enter_context(self.nc.sbuf_tensor(f"{self.tag}_{name}", shape, dt))

    def bank(self, name, shape):
        return self.ctx.enter_context(self.nc.psum_tensor(f"{self.tag}_{name}", shape, FP32))

    def sem(self, name):
        return self.ctx.enter_context(self.nc.semaphore(f"{self.tag}_{name}"))


class Chain:

    def __init__(self, engine, sem):
        self.engine, self.sem, self.n = engine, sem, 0

    def mark(self, ins):
        ins.then_inc(self.sem, 1)
        self.n += 1
        return self.n

    def wait(self, n=None):
        self.engine.wait_ge(self.sem, self.n if n is None else n)

    def step(self, ins):
        self.mark(ins)
        self.wait()

    def restart(self):
        self.wait()
        self.engine.sem_clear(self.sem)
        self.n = 0


TOK_H, TOK_N, TOK_C, TOK_L = 64, 64, 16, 512
GH = 4
GROUPS = 2
TOK_ITERS = TOK_H // (GH * GROUPS)
VCOLS = 64
UROWS = TOK_L // VCOLS
NEUMANN = 4
R_DA, R_DAT, R_DB, R_POW, R_OUT = 4, 5, 6, 7, 16
ROUNDS = 17


def build_tokens(nc, d_u, d_v, d_b, d_c, d_ldt, d_h1):
    with ExitStack() as ctx:
        s = Scope(nc, ctx, "tok")
        u_raw = s.sb("u_raw", [P, GROUPS * GH, P])
        v_raw = s.sb("v_raw", [P, GROUPS * GH, P])
        x = s.sb("x", [P, GROUPS, GH, P])
        xt = s.sb("xt", [P, GROUPS, GH, P])
        f = s.sb("f", [P, GROUPS, GH, P])
        pw = s.sb("pw", [P, GROUPS, GH, P])
        pwt = s.sb("pwt", [P, GROUPS, GH, P])
        vv = s.sb("vv", [P, GROUPS, GH, VCOLS])
        uu = s.sb("uu", [P, GROUPS, GH, UROWS * TOK_C])
        oo = s.sb("oo", [P, GROUPS, GH, VCOLS])
        b_all = s.sb("b_all", [P, TOK_H])
        c_all = s.sb("c_all", [P, TOK_H * TOK_C])
        hdt = s.sb("hdt", [P, TOK_H])
        sgn_u = s.sb("sgn_u", [P, P])
        sgn_v = s.sb("sgn_v", [P, P])
        sgn_c = s.sb("sgn_c", [P, 1])
        ident = s.sb("ident", [P, P])
        ps_p = [s.bank(f"ps_p{g}", [P, GH, P]) for g in range(GROUPS)]
        ps_t = [s.bank(f"ps_t{g}", [P, GH, P]) for g in range(GROUPS)]
        ps_s = [s.bank(f"ps_s{g}", [P, GH, P]) for g in range(GROUPS)]

        params_in = s.sem("params_in")
        raw_in = s.sem("raw_in")
        raw_used = s.sem("raw_used")
        consts = s.sem("consts")
        hdt_done = s.sem("hdt_done")
        x_ready = [s.sem(f"x_ready{g}") for g in range(GROUPS)]
        pe_round = [s.sem(f"pe_round{g}") for g in range(GROUPS)]
        dve_round = [s.sem(f"dve_round{g}") for g in range(GROUPS)]
        act_round = [s.sem(f"act_round{g}") for g in range(GROUPS)]
        da_done = [s.sem(f"da_done{g}") for g in range(GROUPS)]
        out_done = [s.sem(f"out_done{g}") for g in range(GROUPS)]
        dve_own = s.sem("dve_own")
        pool_own = s.sem("pool_own")

        act_rounds = [0, 1, 2, 3, R_DAT] + [R_POW + k for k in range(7)] + [R_OUT]
        ACT_N = len(act_rounds)

        dve_rounds = [r for r in range(ROUNDS) if r not in (R_DA, R_DAT, R_OUT)]
        DVE_N = len(dve_rounds)

        def act_before(r):
            return sum(q < r for q in act_rounds)

        def dve_before(r):
            return sum(q < r for q in dve_rounds)

        with nc.Block() as block:
            @block.sync
            def _(sp):
                sp.dma_start(b_all[:], d_b).then_inc(params_in, 16)
                sp.dma_start(c_all[:], d_c).then_inc(params_in, 16)
                sp.dma_start(hdt[:], d_ldt).then_inc(params_in, 16)
                with sp.Fori(0, TOK_ITERS) as i:
                    sp.wait_ge(raw_used, i * GROUPS)
                    sp.dma_start(u_raw[:], d_u[:, bass.ds(i * (GROUPS * GH), GROUPS * GH), :]).then_inc(raw_in, 16)
                    sp.dma_start(v_raw[:], d_v[:, bass.ds(i * (GROUPS * GH), GROUPS * GH), :]).then_inc(raw_in, 16)
                for g in range(GROUPS):
                    sp.wait_ge(out_done[g], 16 * TOK_ITERS)

            @block.gpsimd
            def _(pool):
                nc.gpsimd.memset(ident[:], 0.0).then_inc(consts, 1)
                nc.gpsimd.memset(sgn_u[:], 1.0).then_inc(consts, 1)
                nc.gpsimd.memset(sgn_v[:], 1.0).then_inc(consts, 1)
                nc.gpsimd.memset(sgn_c[:], 1.0).then_inc(consts, 1)
                pool.wait_ge(consts, 4)
                nc.gpsimd.affine_select(out=ident[:], in_=ident[:], compare_op=ALU.not_equal, fill=1.0,
                                        base=0, pattern=[[-1, P]], channel_multiplier=1).then_inc(consts, 1)
                pool.wait_ge(consts, 5)
                nc.gpsimd.memset(sgn_u[0:64, 64:128], -1.0).then_inc(consts, 1)
                pool.wait_ge(consts, 6)
                nc.gpsimd.memset(sgn_v[64:128, 0:64], -1.0).then_inc(consts, 1)
                nc.gpsimd.memset(sgn_c[64:128, :], -1.0).then_inc(consts, 1)
                pool.wait_ge(consts, 8)
                pool.wait_ge(hdt_done, 2)
                own = Chain(pool, pool_own)
                with pool.Fori(0, TOK_ITERS) as i:
                    pool.wait_ge(raw_in, i * 32 + 32)
                    for g in range(GROUPS):
                        h0 = i * (GROUPS * GH) + g * GH
                        hd = hdt[:, bass.ds(h0, GH)].unsqueeze(2).to_broadcast([P, GH, P])
                        su = sgn_u[:].unsqueeze(1).to_broadcast([P, GH, P])
                        sv = sgn_v[:].unsqueeze(1).to_broadcast([P, GH, P])
                        idb = ident[:].unsqueeze(1).to_broadcast([P, GH, P])
                        pool.wait_ge(da_done[g], i)
                        own.mark(nc.gpsimd.tensor_tensor(u_raw[:, g * GH:(g + 1) * GH, :], u_raw[:, g * GH:(g + 1) * GH, :], hd, ALU.mult))
                        own.mark(nc.gpsimd.tensor_tensor(v_raw[:, g * GH:(g + 1) * GH, :], v_raw[:, g * GH:(g + 1) * GH, :], hd, ALU.mult))
                        own.wait(own.n - 1)
                        own.mark(nc.gpsimd.tensor_tensor(x[:, g], u_raw[:, g * GH:(g + 1) * GH, :], su, ALU.mult))
                        own.wait(own.n - 1)
                        own.mark(nc.gpsimd.tensor_tensor(xt[:, g], v_raw[:, g * GH:(g + 1) * GH, :], sv, ALU.mult))
                        own.wait(own.n)
                        pool.sem_inc(raw_used, 1)
                        nc.gpsimd.tensor_tensor(f[:, g], x[:, g], idb, ALU.add).then_inc(x_ready[g], 1)
                    own.restart()

            @block.tensor
            def _(pe):
                pe.wait_ge(consts, 5)
                pe.wait_ge(params_in, 48)
                mm = nc.tensor.matmul
                with pe.Fori(0, TOK_ITERS) as i:
                    for r in range(ROUNDS):
                        for g in range(GROUPS):
                            h0 = i * (GROUPS * GH) + g * GH
                            if r == 0:
                                pe.wait_ge(x_ready[g], i + 1)
                            pe.wait_ge(dve_round[g], i * DVE_N + dve_before(r))
                            if r == R_DAT:
                                pe.wait_ge(da_done[g], i + 1)
                            pe.wait_ge(act_round[g], i * ACT_N + act_before(r))
                            a, at = (x, xt) if r == 0 else (pw, pwt)
                            square = r < NEUMANN - 1 or R_POW <= r < R_POW + 7
                            m = 1 << (r - R_POW) if r >= R_POW else 0
                            for h in range(GH):
                                if square or r == R_POW + 7:
                                    last = mm(ps_p[g][:, h], at[:, g, h], a[:, g, h], start=True, stop=True)
                                if square or r == NEUMANN - 1:
                                    last = mm(ps_t[g][:, h], a[:, g, h], at[:, g, h], start=True, stop=True)
                                if 1 <= r <= NEUMANN:
                                    last = mm(ps_s[g][:, h], pwt[:, g, h], f[:, g, h], start=True, stop=True)
                                if r == R_DAT:
                                    last = nc.tensor.transpose(ps_t[g][:, h], pw[:, g, h], ident[:])
                                if r == R_DB:
                                    last = mm(ps_s[g][:, h, 0:1], pwt[:, g, h], b_all[:, bass.ds(h0 + h, 1)], start=True, stop=True)
                                if R_POW <= r < R_OUT and m < VCOLS:
                                    last = mm(ps_s[g][:, h, 0:m], pwt[:, g, h], vv[:, g, h, 0:m], start=True, stop=True)
                                if R_POW <= r < R_OUT and m >= VCOLS:
                                    n = m // VCOLS * TOK_C
                                    last = mm(ps_s[g][:, h, 0:n], pw[:, g, h], uu[:, g, h, 0:n], start=True, stop=True)
                                if r == R_OUT:
                                    last = mm(ps_s[g][:, h, 0:VCOLS], uu[:, g, h], vv[:, g, h], start=True, stop=True)
                            last.then_inc(pe_round[g], 1)

            @block.vector
            def _(dve):
                dve.wait_ge(consts, 5)
                dve.wait_ge(params_in, 48)
                dve.wait_ge(hdt_done, 2)
                own = Chain(dve, dve_own)
                with dve.Fori(0, TOK_ITERS) as i:
                    for r in range(ROUNDS):
                        if r in (R_DAT, R_OUT):
                            continue
                        for g in range(GROUPS):
                            h0 = i * (GROUPS * GH) + g * GH
                            dve.wait_ge(pe_round[g], i * ROUNDS + r + 1)
                            m = 1 << (r - R_POW) if r >= R_POW else 0
                            if r < NEUMANN - 1 or R_POW <= r < R_POW + 8:
                                last = nc.vector.tensor_copy(pw[:, g], ps_p[g][:])
                            if 1 <= r <= NEUMANN:
                                last = nc.vector.tensor_tensor(f[:, g], f[:, g], ps_s[g][:], ALU.add)
                            if r == R_DA:
                                own.step(last)
                                nc.vector.scalar_tensor_tensor(
                                    pw[:, g], f[:, g], 2.0, ident[:].unsqueeze(1).to_broadcast([P, GH, P]),
                                    ALU.mult, ALU.subtract).then_inc(da_done[g], 1)
                                continue
                            if r == R_DB:
                                own.step(nc.vector.tensor_tensor(vv[:, g, :, 1:2], ps_s[g][:, :, 0:1],
                                                                 b_all[:, bass.ds(h0, GH)].unsqueeze(2), ALU.add))
                                last = nc.vector.tensor_tensor(vv[:, g, :, 0:1], vv[:, g, :, 1:2],
                                                               hdt[:, bass.ds(h0, GH)].unsqueeze(2), ALU.mult)
                            if R_POW <= r < R_OUT and m < VCOLS:
                                last = nc.vector.tensor_copy(vv[:, g, :, m:2 * m], ps_s[g][:, :, 0:m])
                            if R_POW <= r < R_OUT and m >= VCOLS:
                                n = m // VCOLS * TOK_C
                                last = nc.vector.tensor_copy(uu[:, g, :, n:2 * n], ps_s[g][:, :, 0:n])
                            last.then_inc(dve_round[g], 1)
                    own.restart()

            @block.scalar
            def _(act):
                act.wait_ge(params_in, 48)
                act.wait_ge(consts, 8)
                nc.scalar.activation(hdt[:], hdt[:], ACT.Exp).then_inc(hdt_done, 1)
                act.wait_ge(hdt_done, 1)
                nc.scalar.mul(hdt[:], hdt[:], 0.5).then_inc(hdt_done, 1)
                with act.Fori(0, TOK_ITERS) as i:
                    for r in act_rounds:
                        for g in range(GROUPS):
                            h0 = i * (GROUPS * GH) + g * GH
                            act.wait_ge(pe_round[g], i * ROUNDS + r + 1)
                            if r == R_OUT:
                                act.wait_ge(out_done[g], i * 16)
                                nc.scalar.copy(oo[:, g], ps_s[g][:, :, 0:VCOLS]).then_inc(act_round[g], 1)
                                act.wait_ge(act_round[g], i * ACT_N + ACT_N)
                                act.dma_start(d_h1[:, bass.ds(h0, GH), :], oo[:, g]).then_inc(out_done[g], 16)
                                continue
                            if r == R_DAT:
                                nc.scalar.activation(
                                    uu[:, g, :, 0:TOK_C],
                                    c_all[:, bass.ds(h0 * TOK_C, GH * TOK_C)].rearrange("p (h c) -> p h c", c=TOK_C),
                                    ACT.Copy, scale=sgn_c[:])
                            nc.scalar.copy(pwt[:, g], ps_t[g][:]).then_inc(act_round[g], 1)


D = 512
KD = D // P
SLOTS = 168
SEQ_TOK, SEQ_TXT = 64, 128
SEQ = SEQ_TOK + SEQ_TXT
BATCH = 16
D_IN = 1024
MI = D_IN // P
NH, HP, NS = 16, 64, 64
TAPS = 4
PAD = TAPS - 1
COL_Z, COL_X, COL_B = 0, D_IN, 2 * D_IN
COL_DT, COL_C = COL_B + NS, COL_B + NS + NH
PROJ = COL_C + NS
TB, TC = MI, MI + 1
EPS = 1e-5
E, TOPK, PRIM = 32, 8, 4
SEC = TOPK - PRIM
TOKENS = BATCH * SEQ
ROWS = TOKENS + P
XW = D + E
EXP_TILES = TOKENS // P
SLOT_COLS = E * EXP_TILES + 1
PAIRS = BATCH // 2


def row_chunks(n, size):
    return [(a, min(size, n - a)) for a in range(0, n, size)]


def build_table(nc, win, d_win, d_cat, d_ptab, d_ztab):
    parts = row_chunks(SLOTS, P)
    chunks = row_chunks(PROJ, D)
    with ExitStack() as ctx:
        s = Scope(nc, ctx, "tab")
        cat = s.sb("cat", [P, 2, D])
        ex = s.sb("ex", [P, 2, D])
        xn = s.sb("xn", [P, 2, D])
        xnt = s.sb("xnt", [P, KD, SLOTS])
        zt = s.sb("zt", [P, 2, PROJ])
        nmx = s.sb("nmx", [P, 2])
        sm = s.sb("sm", [P, 2])
        rs = s.sb("rs", [P, 2])
        st = s.sb("st", [P, 2, 6])
        mv = s.sb("mv", [P, 2, 2])
        ve = s.sb("ve", [P, 2])
        rstd = s.sb("rstd", [P, 2])
        mhalf = s.sb("mhalf", [P, 2])
        ident = s.sb("ident", [P, P])
        ps_t = s.bank("ps_t", [P, KD, P])
        ps_t2 = s.bank("ps_t2", [P, KD, P])
        ps_z = [s.bank(f"ps_z{n}", [P, D]) for n in range(4)]
        cat_in = s.sem("cat_in")
        win_in = s.sem("win_in")
        consts = s.sem("consts")
        nmx_done = s.sem("nmx_done")
        ex_done = s.sem("ex_done")
        ve_done = s.sem("ve_done")
        rstd_done = s.sem("rstd_done")
        xn_done = s.sem("xn_done")
        probs_done = s.sem("probs_done")
        t_done = s.sem("t_done")
        xnt_done = s.sem("xnt_done")
        z_done = s.sem("z_done")
        z_read = s.sem("z_read")
        stored = s.sem("stored")
        dve_own = s.sem("dve_own")

        with nc.Block() as block:
            @block.sync
            def _(sp):
                for n, (a, k) in enumerate(parts):
                    sp.dma_start(cat[0:k, n], d_cat[a:a + k, :]).then_inc(cat_in, 16)
                sp.dma_start(win[:], d_win.rearrange("(k p) n -> p k n", p=P)).then_inc(win_in, 16)
                for n, (a, k) in enumerate(parts):
                    sp.wait_ge(probs_done, n + 1)
                    sp.dma_start(d_ptab[a:a + k, :], ex[0:k, n]).then_inc(stored, 16)
                for n, (a, k) in enumerate(parts):
                    sp.wait_ge(z_read, (n + 1) * len(chunks))
                    sp.dma_start(d_ztab[a:a + k, :], zt[0:k, n]).then_inc(stored, 16)
                sp.wait_ge(stored, 64)

            @block.gpsimd
            def _(pool):
                nc.gpsimd.memset(ident[:], 0.0).then_inc(consts, 1)
                nc.gpsimd.memset(mhalf[:], -0.5).then_inc(consts, 1)
                pool.wait_ge(consts, 2)
                nc.gpsimd.affine_select(out=ident[:], in_=ident[:], compare_op=ALU.not_equal, fill=1.0,
                                        base=0, pattern=[[-1, P]], channel_multiplier=1).then_inc(consts, 1)
                for n, (a, k) in enumerate(parts):
                    pool.wait_ge(ve_done, n + 1)
                    nc.gpsimd.tensor_tensor(rstd[0:k, n:n + 1], ve[0:k, n:n + 1], mhalf[0:k, n:n + 1],
                                            ALU.pow).then_inc(rstd_done, 1)

            @block.scalar
            def _(act):
                for n, (a, k) in enumerate(parts):
                    act.wait_ge(nmx_done, n + 1)
                    nc.scalar.activation(ex[0:k, n], cat[0:k, n], ACT.Exp, bias=nmx[0:k, n:n + 1],
                                         accum_out=sm[0:k, n:n + 1]).then_inc(ex_done, 1)
                for n, (a, k) in enumerate(parts):
                    act.wait_ge(t_done, n + 1)
                    nc.scalar.copy(xnt[:, :, a:a + k], (ps_t, ps_t2)[n][:, :, 0:k]).then_inc(xnt_done, 1)

            @block.vector
            def _(dve):
                own = Chain(dve, dve_own)
                for n, (a, k) in enumerate(parts):
                    dve.wait_ge(cat_in, 32)
                    nc.vector.tensor_reduce(nmx[0:k, n:n + 1], cat[0:k, n], AX.X, ALU.max, negate=True).then_inc(nmx_done, 1)
                for n, (a, k) in enumerate(parts):
                    dve.wait_ge(ex_done, n + 1)
                    own.step(nc.vector.reciprocal(rs[0:k, n:n + 1], sm[0:k, n:n + 1]))
                    nc.vector.tensor_scalar(ex[0:k, n], ex[0:k, n], rs[0:k, n:n + 1], None, ALU.mult).then_inc(probs_done, 1)
                    dve.wait_ge(probs_done, n + 1)
                    own.step(nc.vector.bn_stats(st[0:k, n], ex[0:k, n]))
                    own.step(nc.vector.bn_aggr(mv[0:k, n], st[0:k, n]))
                    nc.vector.tensor_scalar(ve[0:k, n:n + 1], mv[0:k, n, 1:2], EPS, None, ALU.add).then_inc(ve_done, 1)
                    dve.wait_ge(rstd_done, n + 1)
                    nc.vector.tensor_scalar(xn[0:k, n], ex[0:k, n], mv[0:k, n, 0:1], rstd[0:k, n:n + 1],
                                            ALU.subtract, ALU.mult).then_inc(xn_done, 1)
                u = 0
                for n, (a, k) in enumerate(parts):
                    for c, w in chunks:
                        u += 1
                        dve.wait_ge(z_done, u)
                        nc.vector.tensor_copy(zt[0:k, n, c:c + w], ps_z[(u - 1) % 4][0:k, 0:w]).then_inc(z_read, 1)

            @block.tensor
            def _(pe):
                pe.wait_ge(consts, 3)
                for n, (a, k) in enumerate(parts):
                    pe.wait_ge(xn_done, n + 1)
                    for t in range(KD):
                        last = nc.tensor.transpose((ps_t, ps_t2)[n][:, t, 0:k], xn[0:k, n, t * P:(t + 1) * P], ident[0:k, 0:k])
                    last.then_inc(t_done, 1)
                pe.wait_ge(win_in, 16)
                u = 0
                for n, (a, k) in enumerate(parts):
                    pe.wait_ge(xnt_done, n + 1)
                    for c, w in chunks:
                        if u >= 4:
                            pe.wait_ge(z_read, u - 3)
                        for t in range(KD):
                            last = nc.tensor.matmul(ps_z[u % 4][0:k, 0:w], xnt[:, t, a:a + k], win[:, t, c:c + w],
                                                    start=t == 0, stop=t == KD - 1)
                        last.then_inc(z_done, 1)
                        u += 1


RING = 3
PROJ_TILES = ([(COL_B, NS + NH, TB), (COL_C, NS, TC)] + [(COL_X + m * P, P, m) for m in range(MI)]
              + [(COL_Z + m * P, P, m) for m in range(MI)])
CONV_TILES = [TB, TC] + list(range(MI))
N_PROJ, N_CONV = len(PROJ_TILES), len(CONV_TILES)
N_XT = 2 * 2 * 2
N_Y = 2 * MI // 2
N_WO = 3
USES_DVE = N_XT + N_Y + N_WO
S0 = P
S1 = SEQ - S0


def build_layer(nc, win, macc, a):
    with ExitStack() as ctx:
        s = Scope(nc, ctx, "lay")
        wout = s.sb("wout", [P, MI, D])
        nw = s.sb("nw", [P, MI])
        gate = s.sb("gate", [P, KD, E])
        sim4 = s.sb("sim4", [P, P])
        cw = s.sb("cw", [P, N_CONV, TAPS])
        cb = s.sb("cb", [P, N_CONV])
        dcol = s.sb("dcol", [P, MI])
        dtb = s.sb("dtb", [NH, 1])
        ea = s.sb("ea", [NH, 1])
        txt = s.sb("txt", [P, BATCH], I32)
        txt_cur = s.sb("txt_cur", [P, 2], I32)
        hres = s.sb("hres", [P, 3, D])
        zt = s.sb("zt", [P, 2, PROJ])
        st = s.sb("st", [P, 6])
        mv = s.sb("mv", [P, 3, 2])
        ve = s.sb("ve", [P, 3])
        rstd = s.sb("rstd", [P, 3])
        mhalf = s.sb("mhalf", [P, 3])
        free = s.sb("free", [P, 3])
        xn = s.sb("xn", [P, D])
        xnt = s.sb("xnt", [P, KD, P])
        zs = s.sb("zs", [P, MI, 2, SEQ])
        xr = s.sb("xr", [P, N_CONV, 2, PAD + SEQ])
        xa = s.sb("xa", [P, N_CONV, 2, SEQ])
        yb = s.sb("yb", [P, MI, 2 * SEQ])
        dtr = s.sb("dtr", [NH, 2, SEQ])
        dtn = s.sb("dtn", [NH, 2, SEQ])
        ones = s.sb("ones", [P, SEQ])
        td_in = s.sb("td_in", [48, 2, SEQ])
        td = s.sb("td", [P, 2, 2, 48])
        m0 = s.sb("m0", [P, 2, NH, SEQ])
        m1 = s.sb("m1", [S1, 2, NH, S1])
        gm = s.sb("gm", [P, 2, SEQ + S1])
        mask = s.sb("mask", [P, SEQ])
        xdt = s.sb("xdt", [P, 2, 2, D_IN])
        ident = s.sb("ident", [P, P])
        lower = s.sb("lower", [P, P], BF16)
        ones_b = s.sb("ones_b", [P, P], BF16)
        ssv = s.sb("ssv", [P, 3])
        rr = s.sb("rr", [P, 3])
        x2 = s.sb("x2", [P, 3, XW])
        ybf = yb[:].rearrange("p m t -> p (m t)")
        x2t = ybf[:, 768:1792].rearrange("p (n k t) -> p n k t", n=2, k=KD)
        oht = ybf[:, 1792:2176].rearrange("p (j t) -> p j t", j=3)
        simr = ybf[:, 2176:2560].rearrange("p (j k e) -> p j k e", j=3, k=SEC)
        prod = ybf[:, 0:3 * TOPK * E]
        iota_e = s.sb("iota_e", [P, E])
        lg = s.sb("lg", [P, 3, E])
        mx = s.sb("mx", [P, 3])
        sm = s.sb("sm", [P, 3])
        top = s.sb("top", [P, 3, TOPK])
        topi = s.sb("topi", [P, 3, TOPK], U32)
        topf = s.sb("topf", [P, 3, TOPK])
        wts = s.sb("wts", [P, 3, TOPK])
        oh = s.sb("oh", [P, 3, TOPK, E])
        sims = s.sb("sims", [P, 3, SEC, PRIM])
        best = s.sb("best", [P, 3, SEC])
        take = s.sb("take", [P, 3, SEC, PRIM])
        rem = s.sb("rem", [P, 3, SEC])
        on = s.sb("on", [P, 3, TOPK])
        moved = s.sb("moved", [P, 3, PRIM])
        mk = s.sb("mk", [P, 3, E], BF16)
        pos = s.sb("pos", [P, 3, E])
        posk = s.sb("posk", [P, 3, TOPK])
        posi = s.sb("posi", [P, 3, TOPK], I32)
        hif = s.sb("hif", [P, 3, TOPK])
        slotf = s.sb("slotf", [P, 3, TOPK])
        slot = s.sb("slot", [P, 3, TOPK], I32)
        tokf = s.sb("tokf", [P, 3])
        toki = s.sb("toki", [P, 3], I32)
        dummy = m0[:].rearrange("p b h t -> p (b h t)")[:, 0:SLOT_COLS].bitcast(I32)
        zero = zt[:, 0, 0:XW]

        ring = [s.bank(f"ring{n}", [P, D]) for n in range(RING)]
        ps_tr = s.bank("ps_tr", [P, KD, P])
        ps_g = s.bank("ps_g", [P, 2, SEQ + S1])
        ps_c = s.bank("ps_c", [P, D])
        ps_q = s.bank("ps_q", [P, 3, P])
        ps_pos = s.bank("ps_pos", [P, 3, E])

        par_in = s.sem("par_in")
        c_own = s.sem("c_own")
        consts = s.sem("consts")
        filled = s.sem("filled")
        w_done = s.sem("w_done")
        tok_in = s.sem("tok_in")
        pool_own = s.sem("pool_own")
        gat_in = s.sem("gat_in")
        ve_done = s.sem("ve_done")
        rstd_done = s.sem("rstd_done")
        xn_done = s.sem("xn_done")
        tr_done = s.sem("tr_done")
        xnt_done = s.sem("xnt_done")
        ring_pe = s.sem("ring_pe")
        ring_act = s.sem("ring_act")
        ring_dve = s.sem("ring_dve")
        dtr_done = s.sem("dtr_done")
        nax_done = s.sem("nax_done")
        sp_done = s.sem("sp_done")
        td_in_done = s.sem("td_in_done")
        cum_out = s.sem("cum_out")
        cum_in = s.sem("cum_in")
        td_tr = s.sem("td_tr")
        td_done = s.sem("td_done")
        conv_done = s.sem("conv_done")
        silu_done = s.sem("silu_done")
        g_done = s.sem("g_done")
        gm_done = s.sem("gm_done")
        e_done = s.sem("e_done")
        m_done = s.sem("m_done")
        xdt_done = s.sem("xdt_done")
        y_pe = s.sem("y_pe")
        y_done = s.sem("y_done")
        sq_done = s.sem("sq_done")
        ss_done = s.sem("ss_done")
        ssv_done = s.sem("ssv_done")
        rr_done = s.sem("rr_done")
        ve2_done = s.sem("ve2_done")
        rstd2_done = s.sem("rstd2_done")
        x2_done = s.sem("x2_done")
        x2tr_done = s.sem("x2tr_done")
        x2t_done = s.sem("x2t_done")
        lg_pe = s.sem("lg_pe")
        lgs_done = s.sem("lgs_done")
        lge_done = s.sem("lge_done")
        oh_done = s.sem("oh_done")
        oht_pe = s.sem("oht_pe")
        oht_done = s.sem("oht_done")
        sim_pe = s.sem("sim_pe")
        mk_done = s.sem("mk_done")
        pos_pe = s.sem("pos_pe")
        macc_done = s.sem("macc_done")
        slot_done = s.sem("slot_done")
        h_out = s.sem("h_out")
        x2_out = s.sem("x2_out")
        scat = s.sem("scat")
        dve_own = s.sem("dve_own")
        act_own = s.sem("act_own")
        N_PAR = 13

        with nc.Block() as block:
            @block.sync
            def _(sp):
                for dst, src in ((wout[:], a["wout"].rearrange("(m p) n -> p m n", p=P)),
                                 (nw[:], a["nw"]), (gate[:], a["gate"].rearrange("(k p) n -> p k n", p=P)),
                                 (cw[:], a["cw"]), (cb[:], a["cb"]), (dcol[:], a["dcol"]),
                                 (dtb[:], a["dtb"]), (ea[:], a["alog"]), (txt[:], a["txt"])):
                    sp.dma_start(dst, src).then_inc(par_in, 16)
                sp.wait_ge(c_own, 13)
                for j in range(SEC):
                    sp.dma_start(sim4[j * E:(j + 1) * E, j * E:(j + 1) * E], a["sim"]).then_inc(par_in, 16)
                sp.dma_start(a["slots"].rearrange("(p c) o -> p (c o)", p=P), dummy).then_inc(filled, 16)
                sp.dma_start(a["xg"][TOKENS:ROWS, :], zero).then_inc(filled, 16)
                sp.dma_start(a["out"][TOKENS:ROWS, :], zero[:, 0:D]).then_inc(filled, 16)
                sp.wait_ge(filled, 48)
                with sp.Fori(0, PAIRS) as i:
                    sp.wait_ge(h_out, i * 64)
                    src = bass.AP(a["h1"].tensor, i * (2 * TOK_H * VCOLS),
                                  [[VCOLS, P], [TOK_C * TOK_H * VCOLS, UROWS], [1, VCOLS]])
                    sp.dma_start(hres[:, 0].rearrange("p (i j) -> p i j", j=VCOLS), src).then_inc(tok_in, 16)
                    sp.wait_ge(td_in_done, i + 1)
                    sp.dma_start(a["cum"].rearrange("b h t -> h b t"), td_in[0:NH]).then_inc(cum_out, 16)
                    sp.wait_ge(cum_out, i * 16 + 16)
                    for b in range(2):
                        sp.dma_start(m0[:, b], a["cum"][b:b + 1].rearrange("b h t -> b (h t)").to_broadcast([P, NH * SEQ]).rearrange("p (h t) -> p h t", h=NH)).then_inc(cum_in, 16)
                        sp.dma_start(m1[:, b], a["cum"][b:b + 1, :, S0:SEQ].to_broadcast([S1, NH, S1])).then_inc(cum_in, 16)
                    out_v = a["out"]
                    sp.wait_ge(x2_done, i * 3 + 3)
                    for b in range(2):
                        sp.dma_start(out_v[bass.ds(i * (2 * SEQ) + b * SEQ, SEQ_TOK), :],
                                     hres[b * SEQ_TOK:(b + 1) * SEQ_TOK, 0]).then_inc(h_out, 16)
                        sp.dma_start(out_v[bass.ds(i * (2 * SEQ) + b * SEQ + SEQ_TOK, SEQ_TXT), :],
                                     hres[:, 1 + b]).then_inc(h_out, 16)
                    sp.wait_ge(mk_done, i + 1)
                    for b in range(2):
                        sp.dma_start(a["xg"][bass.ds(i * (2 * SEQ) + b * SEQ, SEQ_TOK), :],
                                     x2[b * SEQ_TOK:(b + 1) * SEQ_TOK, 0]).then_inc(x2_out, 16)
                        sp.dma_start(a["xg"][bass.ds(i * (2 * SEQ) + b * SEQ + SEQ_TOK, SEQ_TXT), :],
                                     x2[:, 1 + b]).then_inc(x2_out, 16)
                sp.wait_ge(h_out, PAIRS * 64)
                sp.wait_ge(x2_out, PAIRS * 64)

            @block.gpsimd
            def _(pool):
                c = Chain(pool, c_own)
                c.step(nc.gpsimd.memset(ident[:], 0.0))
                c.step(nc.gpsimd.affine_select(out=ident[:], in_=ident[:], compare_op=ALU.not_equal, fill=1.0,
                                               base=0, pattern=[[-1, P]], channel_multiplier=1))
                c.step(nc.gpsimd.memset(mask[:], 1.0))
                c.step(nc.gpsimd.affine_select(out=mask[:], in_=mask[:], compare_op=ALU.is_ge, fill=0.0,
                                               base=0, pattern=[[1, SEQ]], channel_multiplier=-1))
                c.step(nc.gpsimd.memset(lower[:], 1.0))
                c.step(nc.gpsimd.affine_select(out=lower[:], in_=lower[:], compare_op=ALU.is_gt, fill=0.0,
                                               base=0, pattern=[[1, P]], channel_multiplier=-1))
                c.step(nc.gpsimd.memset(ones_b[:], 1.0))
                c.step(nc.gpsimd.memset(zero, 0.0))
                c.step(nc.gpsimd.memset(mhalf[:], -0.5))
                c.step(nc.gpsimd.memset(sim4[:], 0.0))
                c.step(nc.gpsimd.memset(td_in[:], 0.0))
                c.step(nc.gpsimd.memset(xr[:, :, :, 0:PAD], 0.0))
                c.step(nc.gpsimd.iota(dummy, pattern=[[0, SLOT_COLS]], base=TOKENS, channel_multiplier=1))
                c.step(nc.gpsimd.memset(ones[:], 1.0))
                c.step(nc.gpsimd.memset(macc[:], 0.0))
                c.step(nc.gpsimd.iota(iota_e[:], pattern=[[1, E]], base=0, channel_multiplier=0,
                                      allow_small_or_imprecise_dtypes=True))
                c.step(nc.gpsimd.iota(tokf[0:SEQ_TOK, 0:1], pattern=[[0, 1]], base=0, channel_multiplier=1,
                                      allow_small_or_imprecise_dtypes=True))
                c.step(nc.gpsimd.iota(tokf[SEQ_TOK:P, 0:1], pattern=[[0, 1]], base=SEQ, channel_multiplier=1,
                                      allow_small_or_imprecise_dtypes=True))
                c.step(nc.gpsimd.iota(tokf[:, 1:3], pattern=[[SEQ, 2]], base=SEQ_TOK, channel_multiplier=1,
                                      allow_small_or_imprecise_dtypes=True))
                pool.wait_ge(par_in, N_PAR * 16)
                nc.gpsimd.affine_select(out=sim4[:], in_=sim4[:], compare_op=ALU.not_equal, fill=1.0,
                                        base=0, pattern=[[-1, P]], channel_multiplier=1).then_inc(consts, 1)
                pool.wait_ge(filled, 48)
                own = Chain(pool, pool_own)
                with pool.Fori(0, PAIRS) as i:
                    own.step(nc.gpsimd.tensor_copy(txt_cur[:], txt[:, bass.ds(i * 2, 2)]))
                    pool.wait_ge(h_out, i * 64)
                    own.step(nc.gpsimd.tensor_tensor(free[:], mhalf[:], mhalf[:], ALU.mult))
                    for b in range(2):
                        off = bass.IndirectOffsetOnAxis(ap=txt_cur[:, b:b + 1], axis=0)
                        pool.indirect_dma_start(out=zt[:, b], out_offset=None, in_=a["ztab"], in_offset=off,
                                                bounds_check=SLOTS - 1).then_inc(gat_in, 16)
                    for b in range(2):
                        off = bass.IndirectOffsetOnAxis(ap=txt_cur[:, b:b + 1], axis=0)
                        pool.indirect_dma_start(out=hres[:, 1 + b], out_offset=None, in_=a["ptab"], in_offset=off,
                                                bounds_check=SLOTS - 1).then_inc(gat_in, 16)
                    pool.wait_ge(ve_done, i + 1)
                    nc.gpsimd.tensor_tensor(rstd[:, 0:1], ve[:, 0:1], mhalf[:, 0:1], ALU.pow).then_inc(rstd_done, 1)
                    pool.wait_ge(ssv_done, i + 1)
                    nc.gpsimd.tensor_tensor(rr[:], ssv[:], mhalf[:], ALU.pow).then_inc(rr_done, 1)
                    pool.wait_ge(ve2_done, i + 1)
                    nc.gpsimd.tensor_tensor(rstd[:], ve[:], mhalf[:], ALU.pow).then_inc(rstd2_done, 1)
                    pool.wait_ge(slot_done, i + 1)
                    own.step(nc.gpsimd.tensor_tensor(slotf[:], posk[:], on[:], ALU.add))
                    own.step(nc.gpsimd.tensor_copy(slot[:], slotf[:]))
                    for j in range(3):
                        for k in range(TOPK):
                            pool.indirect_dma_start(
                                out=a["slots"], out_offset=bass.IndirectOffsetOnAxis(ap=slot[:, j, k:k + 1], axis=0),
                                in_=toki[:, j:j + 1], in_offset=None,
                                bounds_check=P * SLOT_COLS - 1, oob_is_err=False).then_inc(scat, 16)
                    own.restart()
                pool.wait_ge(scat, PAIRS * 3 * TOPK * 16)

            @block.scalar
            def _(act):
                act.wait_ge(par_in, N_PAR * 16)
                nc.scalar.activation(ea[:], ea[:], ACT.Exp).then_inc(w_done, 1)
                own = Chain(act, act_own)
                with act.Fori(0, PAIRS) as i:
                    act.wait_ge(tr_done, i + 1)
                    nc.scalar.copy(xnt[:], ps_tr[:]).then_inc(xnt_done, 1)
                    for q in range(2 + MI):
                        _, w, m = PROJ_TILES[q]
                        k = min(w, P) if m < MI else NS
                        act.wait_ge(ring_pe, i * (N_PROJ + USES_DVE) + q + 1)
                        bank = ring[q % RING][:, 0:2 * SEQ].rearrange("p (b t) -> p b t", b=2)
                        if m == TB:
                            nc.scalar.copy(dtr[:], bank[NS:NS + NH]).then_inc(dtr_done, 1)
                        nc.scalar.copy(xr[0:k, m, :, PAD:PAD + SEQ], bank[0:k]).then_inc(ring_act, 1)
                        if q == 3:
                            act.wait_ge(nax_done, i + 1)
                            own.step(nc.scalar.activation(dtn[:], dtn[:], ACT.Exp))
                            nc.scalar.activation(dtn[:], dtn[:], ACT.Ln, bias=1.0).then_inc(sp_done, 1)
                    for n in range(N_CONV):
                        if n < MI:
                            q = 2 + MI + n
                            act.wait_ge(ring_pe, i * (N_PROJ + USES_DVE) + q + 1)
                            bank = ring[q % RING][:, 0:2 * SEQ].rearrange("p (b t) -> p b t", b=2)
                            nc.scalar.activation(zs[:, n], bank, ACT.Silu).then_inc(ring_act, 1)
                        m = CONV_TILES[n]
                        k = P if m < MI else NS
                        act.wait_ge(conv_done, i * N_CONV + n + 1)
                        nc.scalar.activation(xa[0:k, m], xa[0:k, m], ACT.Silu).then_inc(silu_done, 1)
                    act.wait_ge(cum_in, i * 64 + 64)
                    act.wait_ge(td_done, i + 1)
                    for b in range(2):
                        for h in range(NH):
                            nc.scalar.activation(m0[:, b, h], m0[:, b, h], ACT.Exp, bias=td[:, b, 0, h:h + 1], scale=-1.0)
                            last = nc.scalar.activation(m1[:, b, h], m1[:, b, h], ACT.Exp, bias=td[0:S1, b, 1, h:h + 1], scale=-1.0)
                        last.then_inc(e_done, 1)
                    act.wait_ge(y_done, i * 2 + 2)
                    nc.scalar.activation(xa[:, 0:MI].rearrange("p m b t -> p m (b t)"), yb[:], ACT.Square).then_inc(sq_done, 1)
                    for j in range(3):
                        act.wait_ge(x2tr_done, i * 3 + j + 1)
                        nc.scalar.copy(x2t[:, j % 2], ps_tr[:]).then_inc(x2t_done, 1)
                    act.wait_ge(lgs_done, i + 1)
                    nc.scalar.activation(lg[:], lg[:], ACT.Exp).then_inc(lge_done, 1)
                    act.wait_ge(oht_pe, i + 1)
                    nc.scalar.copy(oht, ps_q[:]).then_inc(oht_done, 1)
                    own.restart()

            @block.tensor
            def _(pe):
                mm, tr = nc.tensor.matmul, nc.tensor.transpose
                pe.wait_ge(consts, 1)
                pe.wait_ge(w_done, 2)
                USES = N_PROJ + USES_DVE

                def ring_wait(i, u):
                    v = u - RING
                    if 0 <= v < N_PROJ:
                        pe.wait_ge(ring_act, i * N_PROJ + v + 1)
                    elif v >= N_PROJ:
                        pe.wait_ge(ring_dve, i * USES_DVE + v - N_PROJ + 1)

                with pe.Fori(0, PAIRS) as i:
                    pe.wait_ge(xn_done, i + 1)
                    for t in range(KD):
                        last = tr(ps_tr[:, t], xn[:, t * P:(t + 1) * P], ident[:])
                    last.then_inc(tr_done, 1)
                    pe.wait_ge(xnt_done, i + 1)
                    for q, (col, w, m) in enumerate(PROJ_TILES):
                        ring_wait(i, q)
                        if q == 9:
                            pe.wait_ge(td_in_done, i + 1)
                        bank = ring[q % RING][0:w, 0:2 * SEQ].rearrange("p (b t) -> p b t", b=2)
                        for t in range(KD):
                            mm(bank[:, :, 0:SEQ_TOK], win[:, t, col:col + w],
                               xnt[:, t].rearrange("p (b t) -> p b t", b=2), start=t == 0, stop=t == KD - 1)
                        if q == 0:
                            pe.wait_ge(gat_in, i * 64 + 64)
                        for b in range(2):
                            last = tr(bank[:, b, SEQ_TOK:SEQ], zt[:, b, col:col + w], ident[:])
                        last.then_inc(ring_pe, 1)
                        if q == 9:
                            for b in range(2):
                                tr(ps_tr[:, 0, b * 48:(b + 1) * 48], td_in[:, b, 0:S0], ident[0:48, 0:48])
                                last = tr(ps_tr[0:S1, 1, b * 48:(b + 1) * 48], td_in[:, b, S0:SEQ], ident[0:48, 0:48])
                            last.then_inc(td_tr, 1)
                    pe.wait_ge(silu_done, i * N_CONV + 2)
                    for b in range(2):
                        mm(ps_g[:, b, 0:SEQ], xa[0:NS, TB, b, 0:S0], xa[0:NS, TC, b], start=True, stop=True)
                        last = mm(ps_g[0:S1, b, SEQ:SEQ + S1], xa[0:NS, TB, b, S0:SEQ], xa[0:NS, TC, b, S0:SEQ], start=True, stop=True)
                    last.then_inc(g_done, 1)
                    u = N_PROJ
                    pe.wait_ge(silu_done, i * N_CONV + N_CONV)

                    def x_transposes(b, u):
                        for half in range(2):
                            for part, (t0, n) in enumerate(((0, S0), (S0, S1))):
                                if part == 0:
                                    ring_wait(i, u)
                                    ring_wait(i, u + 1)
                                for m in range(4):
                                    last = tr(ring[u % RING][0:n, m * P:(m + 1) * P], xa[:, half * 4 + m, b, t0:t0 + n], ident[:])
                                last.then_inc(ring_pe, 1)
                                u += 1
                        return u

                    def y_products(b, u):
                        pe.wait_ge(m_done, i * 2 + b + 1)
                        for m2 in range(MI // 2):
                            ring_wait(i, u)
                            for m in (2 * m2, 2 * m2 + 1):
                                c0 = (m % 2) * SEQ
                                for h in (2 * m, 2 * m + 1):
                                    p0 = (h % 2) * HP
                                    mm(ring[u % RING][p0:p0 + HP, c0:c0 + SEQ], xdt[:, b, 0, h * HP:(h + 1) * HP],
                                       m0[:, b, h], start=True, stop=False)
                                    last = mm(ring[u % RING][p0:p0 + HP, c0 + S0:c0 + SEQ], xdt[0:S1, b, 1, h * HP:(h + 1) * HP],
                                              m1[:, b, h], start=False, stop=True)
                            last.then_inc(ring_pe, 1)
                            u += 1
                        return u

                    for b in range(2):
                        u = x_transposes(b, u)
                    for b in range(2):
                        u = y_products(b, u)
                    pe.wait_ge(sq_done, i + 1)
                    for j in range(3):
                        for m in range(MI):
                            last = mm(ps_c[:, j:j + 1], xa[:, m].rearrange("p b t -> p (b t)")[:, j * P:(j + 1) * P], ones[:, 0:1], start=m == 0, stop=m == MI - 1)
                    last.then_inc(ss_done, 1)
                    for j in range(3):
                        ring_wait(i, u)
                        for m in range(MI):
                            last = mm(ring[u % RING][:], yb[:, m, j * P:(j + 1) * P], wout[:, m], start=m == 0, stop=m == MI - 1)
                        last.then_inc(ring_pe, 1)
                        u += 1
                    assert u == USES
                    for j in range(3):
                        pe.wait_ge(x2_done, i * 3 + j + 1)
                        if j:
                            pe.wait_ge(x2t_done, i * 3 + j)
                        for t in range(KD):
                            last = tr(ps_tr[:, t], x2[:, j, t * P:(t + 1) * P], ident[:])
                        last.then_inc(x2tr_done, 1)
                        if j == 0:
                            pe.wait_ge(ssv_done, i + 1)
                        pe.wait_ge(x2t_done, i * 3 + j + 1)
                        for t in range(KD):
                            last = mm(ps_c[:, 128 + j * E:128 + (j + 1) * E], x2t[:, j % 2, t], gate[:, t], start=t == 0, stop=t == KD - 1)
                    last.then_inc(lg_pe, 1)
                    pe.wait_ge(oh_done, i + 1)
                    for j in range(3):
                        last = tr(ps_q[:, j], oh[:, j, PRIM:TOPK].rearrange("p k e -> p (k e)"), ident[:])
                    last.then_inc(oht_pe, 1)
                    pe.wait_ge(oht_done, i + 1)
                    for j in range(3):
                        last = mm(ps_q[:, j], oht[:, j], sim4[:], start=True, stop=True)
                    last.then_inc(sim_pe, 1)
                    pe.wait_ge(mk_done, i + 1)
                    for j in range(3):
                        mm(ps_pos[:, j], lower[:], mk[:, j], start=True, stop=False)
                        for q in range(j):
                            mm(ps_pos[:, j], ones_b[:], mk[:, q], start=False, stop=False)
                        last = mm(ps_pos[:, j], ones_b[:], macc[:], start=False, stop=True)
                    last.then_inc(pos_pe, 1)

            @block.vector
            def _(dve):
                v = nc.vector
                own = Chain(dve, dve_own)
                USES = N_PROJ + USES_DVE
                dve.wait_ge(par_in, N_PAR * 16)
                dve.wait_ge(consts, 1)
                v.tensor_tensor(wout[:], wout[:], nw[:].unsqueeze(2).to_broadcast([P, MI, D]), ALU.mult).then_inc(w_done, 1)
                dve.wait_ge(w_done, 2)

                def norm_stats(src, j):
                    own.step(v.bn_stats(st[:], src))
                    own.step(v.bn_aggr(mv[:, j], st[:]))

                with dve.Fori(0, PAIRS) as i:
                    dve.wait_ge(tok_in, i * 16 + 16)
                    norm_stats(hres[:, 0], 0)
                    v.tensor_scalar(ve[:, 0:1], mv[:, 0, 1:2], EPS, None, ALU.add).then_inc(ve_done, 1)
                    dve.wait_ge(rstd_done, i + 1)
                    v.tensor_scalar(xn[:], hres[:, 0], mv[:, 0, 0:1], rstd[:, 0:1], ALU.subtract, ALU.mult).then_inc(xn_done, 1)
                    dve.wait_ge(dtr_done, i + 1)
                    own.step(v.tensor_scalar(dtr[:], dtr[:], dtb[:], None, ALU.add))
                    own.step(v.tensor_scalar(dtn[:], dtr[:], -1.0, None, ALU.mult))
                    v.tensor_tensor(dtn[:], dtn[:], dtr[:], ALU.min).then_inc(nax_done, 1)
                    dve.wait_ge(nax_done, i + 1)

                    def conv(n0):
                        for k in reversed(range(TAPS)):
                            for n in (n0, n0 + 1):
                                m = CONV_TILES[n]
                                r = P if m < MI else NS
                                src = xr[0:r, m, :, k:k + SEQ]
                                if k == TAPS - 1:
                                    ins = v.tensor_scalar(xa[0:r, m], src, cw[0:r, m, k:k + 1], cb[0:r, m:m + 1], ALU.mult, ALU.add)
                                else:
                                    own.wait(own.n if (k, n) == (0, n0 + 1) else own.n - 1)
                                    ins = v.scalar_tensor_tensor(xa[0:r, m], src, cw[0:r, m, k:k + 1], xa[0:r, m], ALU.mult, ALU.add)
                                if k == 0:
                                    ins.then_inc(conv_done, 1)
                                else:
                                    own.mark(ins)

                    dve.wait_ge(ring_act, i * N_PROJ + 2)
                    conv(0)
                    dve.wait_ge(sp_done, i + 1)
                    own.step(v.scalar_tensor_tensor(td_in[32:48], dtr[:], 0.0, dtn[:], ALU.max, ALU.add))
                    own.step(v.tensor_scalar(dtr[:], td_in[32:48], ea[:], None, ALU.mult))
                    for b in range(2):
                        last = v.tensor_tensor_scan(td_in[0:NH, b], ones[0:NH], dtr[:, b], 0.0, ALU.mult, ALU.add)
                    last.then_inc(td_in_done, 1)
                    for n in range(2, N_CONV, 2):
                        dve.wait_ge(ring_act, i * N_PROJ + n + 2)
                        conv(n)
                    dve.wait_ge(td_tr, i + 1)
                    v.tensor_copy(td[:, :, 0], ps_tr[:, 0, 0:96].rearrange("p (b c) -> p b c", b=2))
                    v.tensor_copy(td[0:S1, :, 1], ps_tr[0:S1, 1, 0:96].rearrange("p (b c) -> p b c", b=2)).then_inc(td_done, 1)
                    dve.wait_ge(td_done, i + 1)
                    dve.wait_ge(g_done, i + 1)
                    v.tensor_tensor(gm[:, :, 0:SEQ], ps_g[:, :, 0:SEQ], mask[:].unsqueeze(1).to_broadcast([P, 2, SEQ]), ALU.mult)
                    v.tensor_tensor(gm[0:S1, :, SEQ:SEQ + S1], ps_g[0:S1, :, SEQ:SEQ + S1],
                                    mask[0:S1, 0:S1].unsqueeze(1).to_broadcast([S1, 2, S1]), ALU.mult).then_inc(gm_done, 1)
                    dve.wait_ge(gm_done, i + 1)
                    u = N_PROJ
                    for b in range(2):
                        for half in range(2):
                            for part, n in enumerate((S0, S1)):
                                dve.wait_ge(ring_pe, i * USES + u + 1)
                                dts = td[0:n, b, part, 32 + half * 8:40 + half * 8].unsqueeze(2).to_broadcast([n, 8, HP])
                                v.tensor_tensor(xdt[0:n, b, part, half * 512:(half + 1) * 512].rearrange("p (h c) -> p h c", c=HP),
                                                ring[u % RING][0:n].rearrange("p (h c) -> p h c", c=HP), dts, ALU.mult).then_inc(ring_dve, 1)
                                u += 1
                    for b in range(2):
                        dve.wait_ge(e_done, i * 2 + b + 1)
                        v.scalar_tensor_tensor(m0[:, b], m0[:, b], 1.0, gm[:, b, 0:SEQ].unsqueeze(1).to_broadcast([P, NH, SEQ]),
                                               ALU.min, ALU.mult)
                        v.scalar_tensor_tensor(m1[:, b], m1[:, b], 1.0, gm[0:S1, b, SEQ:SEQ + S1].unsqueeze(1).to_broadcast([S1, NH, S1]),
                                               ALU.min, ALU.mult).then_inc(m_done, 1)
                    for b in range(2):
                        for m2 in range(MI // 2):
                            dve.wait_ge(ring_pe, i * USES + u + 1)
                            for m in (2 * m2, 2 * m2 + 1):
                                c0 = (m % 2) * SEQ
                                last = v.scalar_tensor_tensor(xr[:, m, b, PAD:PAD + SEQ], xa[:, m, b], dcol[:, m:m + 1],
                                                              ring[u % RING][:, c0:c0 + SEQ], ALU.mult, ALU.add)
                            last.then_inc(ring_dve, 1)
                            u += 1
                        dve.wait_ge(ring_dve, i * USES_DVE + u - N_PROJ)
                        v.tensor_tensor(yb[:, :, b * SEQ_TOK:(b + 1) * SEQ_TOK], xr[:, 0:MI, b, PAD:PAD + SEQ_TOK],
                                        zs[:, :, b, 0:SEQ_TOK], ALU.mult)
                        v.tensor_tensor(yb[:, :, (1 + b) * P:(2 + b) * P], xr[:, 0:MI, b, PAD + SEQ_TOK:PAD + SEQ],
                                        zs[:, :, b, SEQ_TOK:SEQ], ALU.mult).then_inc(y_done, 1)
                    dve.wait_ge(ss_done, i + 1)
                    v.tensor_scalar(ssv[:], ps_c[:, 0:3], 1.0 / D_IN, EPS, ALU.mult, ALU.add).then_inc(ssv_done, 1)
                    dve.wait_ge(rr_done, i + 1)
                    dve.wait_ge(gat_in, i * 64 + 64)
                    for j in range(3):
                        dve.wait_ge(ring_pe, i * USES + u + 1)
                        v.scalar_tensor_tensor(hres[:, j], ring[u % RING][:], rr[:, j:j + 1], hres[:, j], ALU.mult, ALU.add).then_inc(ring_dve, 1)
                        dve.wait_ge(ring_dve, i * USES_DVE + u - N_PROJ + 1)
                        own.mark(v.bn_stats(st[:], hres[:, j]))
                        own.wait()
                        own.step(v.bn_aggr(mv[:, j], st[:]))
                        u += 1
                    v.tensor_scalar(ve[:], mv[:, :, 1], EPS, None, ALU.add).then_inc(ve2_done, 1)
                    dve.wait_ge(rstd2_done, i + 1)
                    dve.wait_ge(x2_out, i * 64)
                    for j in range(3):
                        v.tensor_scalar(x2[:, j, 0:D], hres[:, j], mv[:, j, 0:1], rstd[:, j:j + 1], ALU.subtract, ALU.mult).then_inc(x2_done, 1)
                    dve.wait_ge(lg_pe, i + 1)
                    lgp = ps_c[:, 128:128 + 3 * E].rearrange("p (j e) -> p j e", e=E)
                    own.step(v.tensor_reduce(mx[:], lgp, AX.X, ALU.max))
                    v.tensor_tensor(lg[:], lgp, mx[:].unsqueeze(2).to_broadcast([P, 3, E]), ALU.subtract).then_inc(lgs_done, 1)
                    dve.wait_ge(lge_done, i + 1)
                    own.step(v.tensor_reduce(sm[:], lg[:], AX.X, ALU.add))
                    own.step(v.reciprocal(sm[:], sm[:]))
                    own.step(v.tensor_tensor(lg[:], lg[:], sm[:].unsqueeze(2).to_broadcast([P, 3, E]), ALU.mult))
                    for j in range(3):
                        own.step(v.max(top[:, j], lg[:, j]))
                        own.mark(v.max_index(topi[:, j], top[:, j], lg[:, j]))
                    own.step(v.tensor_reduce(sm[:], top[:], AX.X, ALU.add))
                    own.step(v.tensor_copy(topf[:], topi[:]))
                    own.step(v.tensor_scalar(sm[:], sm[:], 1e-12, None, ALU.max))
                    own.step(v.reciprocal(sm[:], sm[:]))
                    own.step(v.tensor_tensor(wts[:], top[:], sm[:].unsqueeze(2).to_broadcast([P, 3, TOPK]), ALU.mult))
                    iot = iota_e[:].unsqueeze(1).to_broadcast([P, 3 * TOPK, E])
                    v.tensor_tensor(oh[:].rearrange("p j k e -> p (j k) e"), iot,
                                    topf[:].rearrange("p j k -> p (j k)").unsqueeze(2).to_broadcast([P, 3 * TOPK, E]),
                                    ALU.is_equal).then_inc(oh_done, 1)
                    dve.wait_ge(oh_done, i + 1)
                    dve.wait_ge(sim_pe, i + 1)
                    own.step(v.tensor_copy(simr.rearrange("p j k e -> p j (k e)"), ps_q[:]))
                    pr = prod[:, 0:SEC * PRIM * E].rearrange("p (a b e) -> p a b e", a=SEC, b=PRIM)
                    for j in range(3):
                        own.step(v.tensor_tensor(pr, simr[:, j].unsqueeze(2).to_broadcast([P, SEC, PRIM, E]),
                                                 oh[:, j, 0:PRIM].unsqueeze(1).to_broadcast([P, SEC, PRIM, E]), ALU.mult))
                        own.step(v.tensor_reduce(sims[:, j], pr, AX.X, ALU.add))
                    own.step(v.tensor_reduce(best[:], sims[:], AX.X, ALU.max))
                    own.step(v.tensor_tensor(take[:], sims[:], best[:].unsqueeze(3).to_broadcast([P, 3, SEC, PRIM]), ALU.is_equal))
                    own.step(v.tensor_scalar(rem[:], best[:], 0.5, None, ALU.is_ge))
                    own.step(v.tensor_scalar(on[:, :, PRIM:TOPK], rem[:], -1.0, 1.0, ALU.mult, ALU.add))
                    for q in range(PRIM):
                        own.step(v.tensor_tensor(take[:, :, :, q], take[:, :, :, q], rem[:], ALU.mult))
                        own.step(v.tensor_tensor(rem[:], rem[:], take[:, :, :, q], ALU.subtract))
                    own.step(v.tensor_tensor(take[:], take[:], wts[:, :, PRIM:TOPK].unsqueeze(3).to_broadcast([P, 3, SEC, PRIM]), ALU.mult))
                    own.step(v.tensor_reduce(moved[:], take[:].rearrange("p j s q -> p j q s"), AX.X, ALU.add))
                    own.step(v.tensor_tensor(wts[:, :, 0:PRIM], wts[:, :, 0:PRIM], moved[:], ALU.add))
                    own.step(v.tensor_tensor(wts[:, :, PRIM:TOPK], wts[:, :, PRIM:TOPK], on[:, :, PRIM:TOPK], ALU.mult))
                    own.step(v.memset(on[:, :, 0:PRIM], 1.0))
                    jk = "p (j k e) -> p (j k) e"
                    pk = prod.rearrange(jk, k=TOPK, e=E)
                    ohk = oh[:].rearrange("p j k e -> p (j k) e")

                    def per_choice(vals):
                        return vals.rearrange("p j k -> p (j k)").unsqueeze(2).to_broadcast([P, 3 * TOPK, E])

                    own.step(v.tensor_tensor(pk, ohk, per_choice(wts[:]), ALU.mult))
                    own.step(v.tensor_reduce(x2[:, :, D:XW], prod.rearrange("p (j k e) -> p j e k", k=TOPK, e=E), AX.X, ALU.add))
                    own.step(v.tensor_tensor(pk, ohk, per_choice(on[:]), ALU.mult))
                    v.tensor_reduce(mk[:], prod.rearrange("p (j k e) -> p j e k", k=TOPK, e=E), AX.X, ALU.max).then_inc(mk_done, 1)
                    dve.wait_ge(pos_pe, i + 1)
                    dve.wait_ge(mk_done, i + 1)
                    own.step(v.tensor_copy(pos[:], ps_pos[:]))
                    for j in range(3):
                        own.step(v.tensor_tensor(macc[:], macc[:], mk[:, j], ALU.add))
                    for j in range(3):
                        own.step(v.tensor_tensor(pk[:, j * TOPK:(j + 1) * TOPK], oh[:, j], pos[:, j].unsqueeze(1).to_broadcast([P, TOPK, E]), ALU.mult))
                    own.step(v.tensor_reduce(posk[:].rearrange("p j k -> p (j k)"), pk, AX.X, ALU.add))
                    dve.wait_ge(scat, i * (3 * TOPK * 16))
                    own.step(v.tensor_copy(posi[:], posk[:]))
                    own.step(v.tensor_scalar(posi[:], posi[:], 7, None, ALU.arith_shift_right))
                    own.step(v.tensor_copy(hif[:], posi[:]))
                    own.step(v.tensor_scalar(posk[:], posk[:], float(SLOT_COLS), None, ALU.mult))
                    own.step(v.scalar_tensor_tensor(posk[:], hif[:], -float(P * SLOT_COLS - 1), posk[:], ALU.mult, ALU.add))
                    own.step(v.scalar_tensor_tensor(posk[:], topf[:], float(EXP_TILES), posk[:], ALU.mult, ALU.add))
                    own.mark(v.tensor_copy(toki[:], tokf[:]))
                    v.tensor_scalar(on[:], on[:], -1.0e6, 1.0e6, ALU.mult, ALU.add).then_inc(slot_done, 1)
                    own.step(v.tensor_scalar(tokf[:], tokf[:], float(2 * SEQ), None, ALU.add))
                    own.restart()


FF = 192
FH = FF // 2
ENTRIES = 256
F_COL, F_W, F_RING, F_CW = range(4)
W_RING = 4
W_DMAS = 2
assert TOKENS * TOPK // P + E + 4 <= ENTRIES


def build_tile_table(nc, macc, tab, thr, iters, d_tab):
    with ExitStack() as ctx:
        s = Scope(nc, ctx, "tbl")
        ones_b = s.sb("ones_b", [P, P], BF16)
        cnt = s.sb("cnt", [P, E])
        cnti = s.sb("cnti", [P, E], I32)
        tiles = s.sb("tiles", [P, E])
        end = s.sb("end", [P, E])
        one = s.sb("one", [P, E])
        gf = s.sb("gf", [P, 2])
        ind = s.sb("ind", [P, 2, E])
        indt = s.sb("indt", [P, 2, E])
        ef = s.sb("ef", [P, 2])
        cs = s.sb("cs", [P, 2])
        neg = s.sb("neg", [P, 2])
        ff = s.sb("ff", [P, 4, 2])
        fi = s.sb("fi", [P, 4, 2], I32)
        thf = s.sb("thf", [1, E])
        itf = s.sb("itf", [1, 1])
        ps = s.bank("ps", [P, E])
        made = s.sem("made")
        counted = s.sem("counted")
        ready = s.sem("ready")
        table_out = s.sem("table_out")
        table_in = s.sem("table_in")
        dve_own = s.sem("dve_own")
        with nc.Block() as block:
            @block.gpsimd
            def _(pool):
                nc.gpsimd.memset(ones_b[:], 1.0).then_inc(made, 1)
                nc.gpsimd.memset(one[:], 1.0).then_inc(made, 1)
                nc.gpsimd.iota(gf[:], pattern=[[P, 2]], base=-1, channel_multiplier=1,
                               allow_small_or_imprecise_dtypes=True).then_inc(made, 1)

            @block.tensor
            def _(pe):
                pe.wait_ge(made, 3)
                nc.tensor.matmul(ps[:], ones_b[:], macc[:], start=True, stop=True).then_inc(counted, 1)

            @block.vector
            def _(dve):
                v = nc.vector
                own = Chain(dve, dve_own)
                dve.wait_ge(made, 3)
                dve.wait_ge(counted, 1)
                own.step(v.tensor_scalar(cnt[:], ps[:], float(P - 1), None, ALU.add))
                own.step(v.tensor_copy(cnti[:], cnt[:]))
                own.step(v.tensor_scalar(cnti[:], cnti[:], 7, None, ALU.arith_shift_right))
                own.step(v.tensor_copy(tiles[:], cnti[:]))
                own.step(v.tensor_tensor_scan(end[:], one[:], tiles[:], 0.0, ALU.mult, ALU.add))
                own.step(v.tensor_tensor(ind[:], end[:].unsqueeze(1).to_broadcast([P, 2, E]),
                                         gf[:].unsqueeze(2).to_broadcast([P, 2, E]), ALU.is_le))
                own.step(v.tensor_reduce(ef[:], ind[:], AX.X, ALU.add))
                own.step(v.tensor_tensor(indt[:], ind[:], tiles[:].unsqueeze(1).to_broadcast([P, 2, E]), ALU.mult))
                own.step(v.tensor_reduce(cs[:], indt[:], AX.X, ALU.add))
                own.step(v.tensor_tensor(cs[:], gf[:], cs[:], ALU.subtract))
                own.step(v.scalar_tensor_tensor(ff[:, F_COL], ef[:], float(EXP_TILES), cs[:], ALU.mult, ALU.add))
                own.step(v.tensor_scalar(neg[:], ff[:, F_COL], 0.0, float(SLOT_COLS), ALU.is_lt, ALU.mult))
                own.step(v.tensor_tensor(ff[:, F_COL], ff[:, F_COL], neg[:], ALU.add))
                own.step(v.tensor_scalar(ff[:, F_COL], ff[:, F_COL], float(SLOT_COLS - 1), None, ALU.min))
                own.step(v.tensor_scalar(ef[:], ef[:], float(E - 1), None, ALU.min))
                own.step(v.tensor_scalar(ff[:, F_W], ef[:], 1.0, float(16 * W_DMAS), ALU.add, ALU.mult))
                own.step(v.tensor_copy(ff[:, F_RING], ef[:]))
                own.step(v.tensor_scalar(ff[:, F_CW], ef[:], float(D), None, ALU.add))
                own.step(v.tensor_copy(fi[:], ff[:]))
                own.step(v.tensor_scalar(fi[:, F_RING], fi[:, F_RING], W_RING - 1, None, ALU.bitwise_and))
                own.step(v.memset(thf[:, 0:W_RING], 0.0))
                own.step(v.tensor_scalar(thf[:, W_RING:E], end[0:1, 0:E - W_RING], 1.0, None, ALU.add))
                own.step(v.tensor_copy(thr[:], thf[:]))
                own.step(v.tensor_scalar(itf[:], end[0:1, E - 1:E], 1.0, None, ALU.add))
                own.step(v.tensor_copy(iters[:], itf[:]))
                v.tensor_scalar(iters[:], iters[:], 1, None, ALU.arith_shift_right).then_inc(ready, 1)
                dve.wait_ge(ready, 1)

            @block.sync
            def _(sp):
                sp.wait_ge(ready, 1)
                with nc.allow_non_contiguous_dma("1024 words of the tile table"):
                    for q in range(4):
                        sp.dma_start(d_tab[q:q + 1, :].rearrange("o (a p) -> p (o a)", p=P), fi[:, q]).then_inc(table_out, 16)
                sp.wait_ge(table_out, 64)
                sp.dma_start(tab[:], d_tab.rearrange("(o q) t -> o q t", o=1)).then_inc(table_in, 16)
                sp.wait_ge(table_in, 16)


def build_experts(nc, tab, thr, iters, a):
    with ExitStack() as ctx:
        s = Scope(nc, ctx, "moe")
        slots = s.sb("slots", [P, SLOT_COLS], I32)
        wgu = s.sb("wgu", [P, W_RING * KD, 2 * FF])
        wd = s.sb("wd", [FH, W_RING * 2, D])
        xg = [s.sb(f"xg{n}", [P, XW]) for n in range(2)]
        xt = [s.sb(f"xt{n}", [P, KD, P]) for n in range(2)]
        sl = [s.sb(f"sl{n}", [P, FF]) for n in range(2)]
        hh = [s.sb(f"hh{n}", [P, FF]) for n in range(2)]
        ht = s.sb("ht", [FH, 2, P])
        yy = [s.sb(f"yy{n}", [P, D]) for n in range(2)]
        idx_g = [s.sb(f"idx_g{n}", [P, 1], I32) for n in range(2)]
        idx_t = s.sb("idx_t", [P, 1], I32)
        zero_i = s.sb("zero_i", [P, 1], I32)
        idx_s = [s.sb(f"idx_s{n}", [P, 1], I32) for n in range(2)]
        ident = s.sb("ident", [P, P])
        ps_gu = [s.bank(f"ps_gu{n}", [P, 2 * FF]) for n in range(2)]
        ps_xt = s.bank("ps_xt", [P, KD, P])
        ps_y = s.bank("ps_y", [P, D])
        ps_ht = s.bank("ps_ht", [P, 2, P])

        slots_in = s.sem("slots_in")
        w_in = s.sem("w_in")
        made = s.sem("made")
        gathered = [s.sem(f"gathered{n}") for n in range(2)]
        added = [s.sem(f"added{n}") for n in range(2)]
        idx_own = s.sem("idx_own")
        t_pe = s.sem("t_pe")
        up_pe = s.sem("up_pe")
        down_pe = s.sem("down_pe")
        ht_pe = s.sem("ht_pe")
        xt_act = s.sem("xt_act")
        sl_act = s.sem("sl_act")
        h_dve = s.sem("h_dve")
        y_dve = s.sem("y_dve")
        ht_dve = s.sem("ht_dve")

        def entry(eng, field, t, hi):
            return eng.value_load(tab[0:1, field, bass.ds(t, 1)], min_val=0, max_val=hi)

        with nc.Block() as block:
            @block.sync
            def _(sp):
                sp.dma_start(slots[:], a["slots"].rearrange("(p c) o -> p (c o)", p=P)).then_inc(slots_in, 16)
                for r in range(W_RING):
                    if r:
                        sp.wait_ge(w_in, 16 * W_DMAS * r)
                    sp.dma_start(wgu[:, r * KD:(r + 1) * KD], a["wgu"][r]).then_inc(w_in, 16)
                    sp.dma_start(wd[:, r * 2:(r + 1) * 2], a["wd"][r]).then_inc(w_in, 16)
                with sp.Fori(0, E // W_RING - 1) as q:
                    for r in range(W_RING):
                        e = q * W_RING + W_RING + r
                        room = sp.value_load(thr[0:1, bass.ds(e, 1)], min_val=1, max_val=ENTRIES)
                        sp.wait_ge(w_in, e * (16 * W_DMAS))
                        sp.wait_ge(down_pe, room)
                        sp.dma_start(wgu[:, r * KD:(r + 1) * KD], a["wgu"][bass.ds(e, 1)].rearrange("o p k n -> p (o k) n")).then_inc(w_in, 16)
                        sp.dma_start(wd[:, r * 2:(r + 1) * 2], a["wd"][bass.ds(e, 1)].rearrange("o p k n -> p (o k) n")).then_inc(w_in, 16)
                sp.wait_ge(w_in, 16 * W_DMAS * E)

            @block.gpsimd
            def _(pool):
                nc.gpsimd.memset(ident[:], 0.0).then_inc(made, 1)
                pool.wait_ge(made, 1)
                nc.gpsimd.affine_select(out=ident[:], in_=ident[:], compare_op=ALU.not_equal, fill=1.0,
                                        base=0, pattern=[[-1, P]], channel_multiplier=1).then_inc(made, 1)
                nc.gpsimd.memset(zero_i[:], 0).then_inc(made, 1)
                pool.wait_ge(made, 3)
                pool.wait_ge(slots_in, 16)
                own = Chain(pool, idx_own)

                def gather(t, n):
                    col = entry(pool, F_COL, t, SLOT_COLS - 1)
                    own.step(nc.gpsimd.tensor_copy(idx_g[n][:], slots[:, bass.ds(col, 1)]))
                    pool.indirect_dma_start(out=xg[n][:], out_offset=None, in_=a["xg"],
                                            in_offset=bass.IndirectOffsetOnAxis(ap=idx_g[n][:, 0:1], axis=0),
                                            bounds_check=ROWS - 1).then_inc(gathered[n], 16)

                def scatter(t, n, y_count):
                    col = entry(pool, F_COL, t, SLOT_COLS - 1)
                    own.step(nc.gpsimd.tensor_copy(idx_t[:], slots[:, bass.ds(col, 1)]))
                    pool.wait_ge(y_dve, y_count)
                    own.step(nc.gpsimd.tensor_tensor(idx_s[n][:], idx_t[:], zero_i[:], ALU.add))
                    pool.indirect_dma_start(out=a["out"], out_offset=bass.IndirectOffsetOnAxis(ap=idx_s[n][:, 0:1], axis=0),
                                            in_=yy[n][:], in_offset=None, bounds_check=ROWS - 1,
                                            compute_op=ALU.add).then_inc(added[n], 16)

                gather(1, 0)
                gather(2, 1)
                own.restart()
                iters_r = pool.value_load(iters[0:1, 0:1], min_val=1, max_val=ENTRIES // 2 - 2)
                with pool.Fori(0, iters_r) as i:
                    for n in range(2):
                        pool.wait_ge(h_dve, i * 2 + n + 1)
                        gather(i * 2 + n + 3, n)
                        if n == 0:
                            pool.wait_ge(added[1], i * 16)
                        else:
                            pool.wait_ge(added[0], i * 16 + 16)
                        scatter(i * 2 + n, n, i * 2 + n + 1)
                    own.restart()
                pool.wait_ge(added[1], iters_r * 16)
                scatter(iters_r * 2, 0, iters_r * 2 + 1)
                pool.wait_ge(added[0], iters_r * 16 + 16)
                for n in range(2):
                    pool.wait_ge(gathered[n], iters_r * 16 + 16)

            @block.scalar
            def _(act):
                iters_r = act.value_load(iters[0:1, 0:1], min_val=1, max_val=ENTRIES // 2 - 2)
                act.wait_ge(t_pe, 1)
                nc.scalar.copy(xt[0][:], ps_xt[:]).then_inc(xt_act, 1)
                with act.Fori(0, iters_r) as i:
                    for n in range(2):
                        act.wait_ge(up_pe, i * 2 + n + 1)
                        nc.scalar.activation(sl[n][:], ps_gu[n][:, 0:FF], ACT.Silu).then_inc(sl_act, 1)
                        act.wait_ge(t_pe, i * 2 + n + 2)
                        nc.scalar.copy(xt[1 - n][:], ps_xt[:]).then_inc(xt_act, 1)

            @block.vector
            def _(dve):
                v = nc.vector
                iters_r = dve.value_load(iters[0:1, 0:1], min_val=1, max_val=ENTRIES // 2 - 2)
                v.memset(ht[:], 0.0).then_inc(ht_dve, 1)
                with dve.Fori(0, iters_r) as i:
                    for n in range(2):
                        cw = entry(dve, F_CW, i * 2 + n + 1, XW - 1)
                        dve.wait_ge(sl_act, i * 2 + n + 1)
                        v.scalar_tensor_tensor(hh[n][:], sl[n][:], xg[n][:, bass.ds(cw, 1)], ps_gu[n][:, FF:2 * FF],
                                               ALU.mult, ALU.mult).then_inc(h_dve, 1)
                        dve.wait_ge(down_pe, i * 2 + n + 1)
                        dve.wait_ge(added[n], i * 16)
                        v.tensor_copy(yy[n][:], ps_y[:]).then_inc(y_dve, 1)
                        dve.wait_ge(ht_pe, i * 2 + n + 1)
                        v.tensor_copy(ht[:], ps_ht[0:FH]).then_inc(ht_dve, 1)
                dve.wait_ge(down_pe, iters_r * 2 + 1)
                dve.wait_ge(added[0], iters_r * 16)
                v.tensor_copy(yy[0][:], ps_y[:]).then_inc(y_dve, 1)

            @block.tensor
            def _(pe):
                mm, tr = nc.tensor.matmul, nc.tensor.transpose
                iters_r = pe.value_load(iters[0:1, 0:1], min_val=1, max_val=ENTRIES // 2 - 2)
                pe.wait_ge(made, 3)
                pe.wait_ge(gathered[0], 16)
                for t in range(KD):
                    last = tr(ps_xt[:, t], xg[0][:, t * P:(t + 1) * P], ident[:])
                last.then_inc(t_pe, 1)

                def down(t, ht_count):
                    r = entry(pe, F_RING, t, W_RING - 1)
                    pe.wait_ge(ht_dve, ht_count)
                    for q in range(2):
                        last = mm(ps_y[:], ht[:, q], wd[:, bass.ds(r * 2 + q, 1)].rearrange("p o n -> p (o n)"), start=q == 0, stop=q == 1)
                    last.then_inc(down_pe, 1)

                with pe.Fori(0, iters_r) as i:
                    for n in range(2):
                        arrivals = entry(pe, F_W, i * 2 + n + 1, 16 * W_DMAS * E)
                        r = entry(pe, F_RING, i * 2 + n + 1, W_RING - 1)
                        pe.wait_ge(w_in, arrivals)
                        pe.wait_ge(xt_act, i * 2 + n + 1)
                        for t in range(KD):
                            last = mm(ps_gu[n][:], xt[n][:, t], wgu[:, bass.ds(r * KD + t, 1)].rearrange("p o n -> p (o n)"), start=t == 0, stop=t == KD - 1)
                        last.then_inc(up_pe, 1)
                        pe.wait_ge(gathered[1 - n], i * 16 + (32 if n else 16))
                        for t in range(KD):
                            last = tr(ps_xt[:, t], xg[1 - n][:, t * P:(t + 1) * P], ident[:])
                        last.then_inc(t_pe, 1)
                        down(i * 2 + n, i * 2 + n + 1)
                        pe.wait_ge(h_dve, i * 2 + n + 1)
                        for q in range(2):
                            last = tr(ps_ht[0:FH, q], hh[n][:, q * FH:(q + 1) * FH], ident[:])
                        last.then_inc(ht_pe, 1)
                down(iters_r * 2, iters_r * 2 + 1)


INPUTS = ("tok_u", "tok_v", "tok_b", "tok_c", "tok_ldt", "win", "cat", "wout", "nw", "gate", "cw", "cb", "dcol",
          "dtb", "alog", "txt", "sim", "wgu", "wd")


def build(nc, a):
    def scratch(name, shape, dt=FP32):
        a[name] = nc.dram_tensor(f"scratch_{name}", shape, dt, kind="Internal").ap()

    scratch("h1", (UROWS * TOK_C, TOK_H, VCOLS))
    scratch("ptab", (SLOTS, D))
    scratch("ztab", (SLOTS, PROJ))
    scratch("cum", (2, NH, SEQ))
    scratch("xg", (ROWS, XW))
    scratch("slots", (P * SLOT_COLS, 1), I32)
    scratch("tab", (4, ENTRIES), I32)
    build_tokens(nc, a["tok_u"], a["tok_v"], a["tok_b"], a["tok_c"], a["tok_ldt"], a["h1"])
    with nc.sbuf_tensor("macc", [P, E], BF16) as macc:
        with nc.sbuf_tensor("win_sb", [P, KD, PROJ], FP32) as win:
            build_table(nc, win, a["win"], a["cat"], a["ptab"], a["ztab"])
            build_layer(nc, win, macc, a)
        with (nc.sbuf_tensor("tile_tab", [1, 4, ENTRIES], I32) as tab, nc.sbuf_tensor("room", [1, E], I32) as thr,
              nc.sbuf_tensor("iters", [1, 1], I32) as iters):
            build_tile_table(nc, macc, tab, thr, iters, a["tab"])
            build_experts(nc, tab, thr, iters, a)


def kernel(**inputs):
    import numpy as np
    import concourse.bacc as bacc
    from concourse.bass_utils import run_bass_kernel_spmd

    x = {k: np.asarray(v) for k, v in inputs.items()}

    def embedding(re, im):
        m = np.concatenate([np.concatenate([re, im], 2), np.concatenate([im, re], 2)], 1)
        return m.transpose(1, 0, 2)

    re, im = x["L0_tok_A"][..., 0], x["L0_tok_A"][..., 1]
    w_in = x["L0_attn_W_in"]
    bc = 2 * D_IN
    w_in = np.concatenate([w_in[:bc + NS], w_in[bc + 2 * NS:], w_in[bc + NS:bc + 2 * NS]])
    conv_w, conv_b = x["L0_attn_conv_w"], x["L0_attn_conv_b"]
    cw = np.zeros((P, N_CONV, TAPS), np.float32)
    cb = np.zeros((P, N_CONV), np.float32)
    cw[:, :MI] = conv_w[:D_IN].reshape(MI, P, TAPS).transpose(1, 0, 2)
    cb[:, :MI] = conv_b[:D_IN].reshape(MI, P).T
    for m, c0 in ((TB, D_IN), (TC, D_IN + NS)):
        cw[:NS, m] = conv_w[c0:c0 + NS]
        cb[:NS, m] = conv_b[c0:c0 + NS]
    arrays = {
        "tok_u": embedding(re, im),
        "tok_v": embedding(re.transpose(0, 2, 1), im.transpose(0, 2, 1)),
        "tok_b": x["L0_tok_B"].transpose(2, 1, 0).reshape(P, TOK_H),
        "tok_c": x["x"].transpose(3, 2, 1, 0).reshape(P, TOK_H * TOK_C),
        "tok_ldt": np.tile(x["L0_tok_log_dt"].reshape(1, TOK_H), (P, 1)),
        "win": w_in.T,
        "cat": x["L0_txt_catid_time_matrix"],
        "wout": x["L0_attn_W_out"].T,
        "nw": x["L0_attn_norm_w"].reshape(MI, P).T,
        "gate": x["L0_ffn_gate_weight"].T,
        "cw": cw, "cb": cb,
        "dcol": np.repeat(x["L0_attn_D"], HP).reshape(MI, P).T,
        "dtb": x["L0_attn_dt_bias"].reshape(NH, 1),
        "alog": x["L0_attn_A_log"].reshape(NH, 1),
        "txt": x["x_txt"].T,
        "sim": x["L0_ffn_similarity"],
        "wgu": x["L0_ffn_gate_up_proj"].reshape(E, 2 * FF, KD, P).transpose(0, 3, 2, 1),
        "wd": x["L0_ffn_down_proj"].reshape(E, D, 2, FH).transpose(0, 3, 2, 1),
    }
    nc = bacc.Bacc("TRN2", target_bir_lowering=False, num_devices=1)
    fed, aps = {}, {}
    for name in INPUTS:
        v = np.ascontiguousarray(arrays[name])
        fed[f"in_{name}"] = v
        aps[name] = nc.dram_tensor(f"in_{name}", v.shape, mybir.dt.from_np(v.dtype), kind="ExternalInput").ap()
    aps["out"] = nc.dram_tensor("out_h", (ROWS, D), FP32, kind="ExternalOutput").ap()
    build(nc, aps)
    r = run_bass_kernel_spmd(nc, [fed], core_ids=[0])
    return r.results[0]["out_h"][:TOKENS].reshape(BATCH, SEQ, D)
```

```python
import concourse.bass as bass
from concourse import mybir
from contextlib import ExitStack

FP32 = mybir.dt.float32
BF16 = mybir.dt.bfloat16
I32 = mybir.dt.int32
U32 = mybir.dt.uint32
ALU = mybir.AluOpType
ACT = mybir.ActivationFunctionType
AX = mybir.AxisListType
P = 128


class Scope:

    def __init__(self, nc, ctx, tag):
        self.nc, self.ctx, self.tag = nc, ctx, tag

    def sb(self, name, shape, dt=FP32):
        return self.ctx.enter_context(self.nc.sbuf_tensor(f"{self.tag}_{name}", shape, dt))

    def bank(self, name, shape):
        return self.ctx.enter_context(self.nc.psum_tensor(f"{self.tag}_{name}", shape, FP32))

    def sem(self, name):
        return self.ctx.enter_context(self.nc.semaphore(f"{self.tag}_{name}"))


class Chain:

    def __init__(self, engine, sem):
        self.engine, self.sem, self.n = engine, sem, 0

    def mark(self, ins):
        ins.then_inc(self.sem, 1)
        self.n += 1
        return self.n

    def wait(self, n=None):
        self.engine.wait_ge(self.sem, self.n if n is None else n)

    def step(self, ins):
        self.mark(ins)
        self.wait()

    def restart(self):
        self.wait()
        self.engine.sem_clear(self.sem)
        self.n = 0


def wait_before(engine, sem, count):
    if not isinstance(count, int) or count > 0:
        engine.wait_ge(sem, count)


TOK_H, TOK_N, TOK_C, TOK_L = 64, 64, 16, 512
GH = 4
GROUPS = 2
TOK_ITERS = TOK_H // (GH * GROUPS)
VCOLS = 64
UROWS = TOK_L // VCOLS
NEUMANN = 4
R_DA, R_DAT, R_DB, R_POW, R_OUT = 4, 5, 6, 7, 16
ROUNDS = 17


def build_tokens(nc, d_u, d_v, d_b, d_c, d_ldt, d_h1):
    with ExitStack() as ctx:
        s = Scope(nc, ctx, "tok")
        u_raw = s.sb("u_raw", [P, GROUPS * GH, P])
        v_raw = s.sb("v_raw", [P, GROUPS * GH, P])
        x = s.sb("x", [P, GROUPS, GH, P])
        xt = s.sb("xt", [P, GROUPS, GH, P])
        f = s.sb("f", [P, GROUPS, GH, P])
        pw = s.sb("pw", [P, GROUPS, GH, P])
        pwt = s.sb("pwt", [P, GROUPS, GH, P])
        vv = s.sb("vv", [P, GROUPS, GH, VCOLS])
        uu = s.sb("uu", [P, GROUPS, GH, UROWS * TOK_C])
        oo = s.sb("oo", [P, GROUPS, GH, VCOLS])
        b_all = s.sb("b_all", [P, TOK_H])
        c_all = s.sb("c_all", [P, TOK_H * TOK_C])
        hdt = s.sb("hdt", [P, TOK_H])
        sgn_u = s.sb("sgn_u", [P, P])
        sgn_v = s.sb("sgn_v", [P, P])
        sgn_c = s.sb("sgn_c", [P, 1])
        ident = s.sb("ident", [P, P])
        ps_p = [s.bank(f"ps_p{g}", [P, GH, P]) for g in range(GROUPS)]
        ps_t = [s.bank(f"ps_t{g}", [P, GH, P]) for g in range(GROUPS)]
        ps_s = [s.bank(f"ps_s{g}", [P, GH, P]) for g in range(GROUPS)]

        params_in = s.sem("params_in")
        raw_in = s.sem("raw_in")
        raw_used = s.sem("raw_used")
        consts = s.sem("consts")
        hdt_done = s.sem("hdt_done")
        x_ready = [s.sem(f"x_ready{g}") for g in range(GROUPS)]
        pe_round = [s.sem(f"pe_round{g}") for g in range(GROUPS)]
        dve_round = [s.sem(f"dve_round{g}") for g in range(GROUPS)]
        act_round = [s.sem(f"act_round{g}") for g in range(GROUPS)]
        da_done = [s.sem(f"da_done{g}") for g in range(GROUPS)]
        out_done = [s.sem(f"out_done{g}") for g in range(GROUPS)]
        dve_own = s.sem("dve_own")
        pool_own = s.sem("pool_own")

        act_rounds = [0, 1, 2, 3, R_DAT] + [R_POW + k for k in range(7)] + [R_OUT]
        ACT_N = len(act_rounds)

        dve_rounds = [r for r in range(ROUNDS) if r not in (R_DA, R_DAT, R_OUT)]
        DVE_N = len(dve_rounds)

        def act_before(r):
            return sum(q < r for q in act_rounds)

        def dve_before(r):
            return sum(q < r for q in dve_rounds)

        with nc.Block() as block:
            @block.sync
            def _(sp):
                sp.dma_start(b_all[:], d_b).then_inc(params_in, 16)
                sp.dma_start(c_all[:], d_c).then_inc(params_in, 16)
                sp.dma_start(hdt[:], d_ldt).then_inc(params_in, 16)
                with sp.Fori(0, TOK_ITERS) as i:
                    sp.wait_ge(raw_used, i * GROUPS)
                    sp.dma_start(u_raw[:], d_u[:, bass.ds(i * (GROUPS * GH), GROUPS * GH), :]).then_inc(raw_in, 16)
                    sp.dma_start(v_raw[:], d_v[:, bass.ds(i * (GROUPS * GH), GROUPS * GH), :]).then_inc(raw_in, 16)
                for g in range(GROUPS):
                    sp.wait_ge(out_done[g], 16 * TOK_ITERS)

            @block.gpsimd
            def _(pool):
                nc.gpsimd.memset(ident[:], 0.0).then_inc(consts, 1)
                nc.gpsimd.memset(sgn_u[:], 1.0).then_inc(consts, 1)
                nc.gpsimd.memset(sgn_v[:], 1.0).then_inc(consts, 1)
                nc.gpsimd.memset(sgn_c[:], 1.0).then_inc(consts, 1)
                pool.wait_ge(consts, 4)
                nc.gpsimd.affine_select(out=ident[:], in_=ident[:], compare_op=ALU.not_equal, fill=1.0,
                                        base=0, pattern=[[-1, P]], channel_multiplier=1).then_inc(consts, 1)
                pool.wait_ge(consts, 5)
                nc.gpsimd.memset(sgn_u[0:64, 64:128], -1.0).then_inc(consts, 1)
                pool.wait_ge(consts, 6)
                nc.gpsimd.memset(sgn_v[64:128, 0:64], -1.0).then_inc(consts, 1)
                nc.gpsimd.memset(sgn_c[64:128, :], -1.0).then_inc(consts, 1)
                pool.wait_ge(consts, 8)
                pool.wait_ge(hdt_done, 2)
                own = Chain(pool, pool_own)
                with pool.Fori(0, TOK_ITERS) as i:
                    pool.wait_ge(raw_in, i * 32 + 32)
                    for g in range(GROUPS):
                        h0 = i * (GROUPS * GH) + g * GH
                        hd = hdt[:, bass.ds(h0, GH)].unsqueeze(2).to_broadcast([P, GH, P])
                        su = sgn_u[:].unsqueeze(1).to_broadcast([P, GH, P])
                        sv = sgn_v[:].unsqueeze(1).to_broadcast([P, GH, P])
                        idb = ident[:].unsqueeze(1).to_broadcast([P, GH, P])
                        pool.wait_ge(da_done[g], i)
                        own.mark(nc.gpsimd.tensor_tensor(u_raw[:, g * GH:(g + 1) * GH, :], u_raw[:, g * GH:(g + 1) * GH, :], hd, ALU.mult))
                        own.mark(nc.gpsimd.tensor_tensor(v_raw[:, g * GH:(g + 1) * GH, :], v_raw[:, g * GH:(g + 1) * GH, :], hd, ALU.mult))
                        own.wait(own.n - 1)
                        own.mark(nc.gpsimd.tensor_tensor(x[:, g], u_raw[:, g * GH:(g + 1) * GH, :], su, ALU.mult))
                        own.wait(own.n - 1)
                        own.mark(nc.gpsimd.tensor_tensor(xt[:, g], v_raw[:, g * GH:(g + 1) * GH, :], sv, ALU.mult))
                        own.wait(own.n)
                        pool.sem_inc(raw_used, 1)
                        nc.gpsimd.tensor_tensor(f[:, g], x[:, g], idb, ALU.add).then_inc(x_ready[g], 1)
                    own.restart()

            @block.tensor
            def _(pe):
                pe.wait_ge(consts, 5)
                pe.wait_ge(params_in, 48)
                mm = nc.tensor.matmul
                with pe.Fori(0, TOK_ITERS) as i:
                    for r in range(ROUNDS):
                        for g in range(GROUPS):
                            h0 = i * (GROUPS * GH) + g * GH
                            if r == 0:
                                pe.wait_ge(x_ready[g], i + 1)
                            pe.wait_ge(dve_round[g], i * DVE_N + dve_before(r))
                            if r == R_DAT:
                                pe.wait_ge(da_done[g], i + 1)
                            pe.wait_ge(act_round[g], i * ACT_N + act_before(r))
                            a, at = (x, xt) if r == 0 else (pw, pwt)
                            square = r < NEUMANN - 1 or R_POW <= r < R_POW + 7
                            m = 1 << (r - R_POW) if r >= R_POW else 0
                            for h in range(GH):
                                if square or r == R_POW + 7:
                                    last = mm(ps_p[g][:, h], at[:, g, h], a[:, g, h], start=True, stop=True)
                                if square or r == NEUMANN - 1:
                                    last = mm(ps_t[g][:, h], a[:, g, h], at[:, g, h], start=True, stop=True)
                                if 1 <= r <= NEUMANN:
                                    last = mm(ps_s[g][:, h], pwt[:, g, h], f[:, g, h], start=True, stop=True)
                                if r == R_DAT:
                                    last = nc.tensor.transpose(ps_t[g][:, h], pw[:, g, h], ident[:])
                                if r == R_DB:
                                    last = mm(ps_s[g][:, h, 0:1], pwt[:, g, h], b_all[:, bass.ds(h0 + h, 1)], start=True, stop=True)
                                if R_POW <= r < R_OUT and m < VCOLS:
                                    last = mm(ps_s[g][:, h, 0:m], pwt[:, g, h], vv[:, g, h, 0:m], start=True, stop=True)
                                if R_POW <= r < R_OUT and m >= VCOLS:
                                    n = m // VCOLS * TOK_C
                                    last = mm(ps_s[g][:, h, 0:n], pw[:, g, h], uu[:, g, h, 0:n], start=True, stop=True)
                                if r == R_OUT:
                                    last = mm(ps_s[g][:, h, 0:VCOLS], uu[:, g, h], vv[:, g, h], start=True, stop=True)
                            last.then_inc(pe_round[g], 1)

            @block.vector
            def _(dve):
                dve.wait_ge(consts, 5)
                dve.wait_ge(params_in, 48)
                dve.wait_ge(hdt_done, 2)
                own = Chain(dve, dve_own)
                with dve.Fori(0, TOK_ITERS) as i:
                    for r in range(ROUNDS):
                        if r in (R_DAT, R_OUT):
                            continue
                        for g in range(GROUPS):
                            h0 = i * (GROUPS * GH) + g * GH
                            dve.wait_ge(pe_round[g], i * ROUNDS + r + 1)
                            m = 1 << (r - R_POW) if r >= R_POW else 0
                            if r < NEUMANN - 1 or R_POW <= r < R_POW + 8:
                                last = nc.vector.tensor_copy(pw[:, g], ps_p[g][:])
                            if 1 <= r <= NEUMANN:
                                last = nc.vector.tensor_tensor(f[:, g], f[:, g], ps_s[g][:], ALU.add)
                            if r == R_DA:
                                own.step(last)
                                nc.vector.scalar_tensor_tensor(
                                    pw[:, g], f[:, g], 2.0, ident[:].unsqueeze(1).to_broadcast([P, GH, P]),
                                    ALU.mult, ALU.subtract).then_inc(da_done[g], 1)
                                continue
                            if r == R_DB:
                                own.step(nc.vector.tensor_tensor(vv[:, g, :, 1:2], ps_s[g][:, :, 0:1],
                                                                 b_all[:, bass.ds(h0, GH)].unsqueeze(2), ALU.add))
                                last = nc.vector.tensor_tensor(vv[:, g, :, 0:1], vv[:, g, :, 1:2],
                                                               hdt[:, bass.ds(h0, GH)].unsqueeze(2), ALU.mult)
                            if R_POW <= r < R_OUT and m < VCOLS:
                                last = nc.vector.tensor_copy(vv[:, g, :, m:2 * m], ps_s[g][:, :, 0:m])
                            if R_POW <= r < R_OUT and m >= VCOLS:
                                n = m // VCOLS * TOK_C
                                last = nc.vector.tensor_copy(uu[:, g, :, n:2 * n], ps_s[g][:, :, 0:n])
                            last.then_inc(dve_round[g], 1)
                    own.restart()

            @block.scalar
            def _(act):
                act.wait_ge(params_in, 48)
                act.wait_ge(consts, 8)
                nc.scalar.activation(hdt[:], hdt[:], ACT.Exp).then_inc(hdt_done, 1)
                act.wait_ge(hdt_done, 1)
                nc.scalar.mul(hdt[:], hdt[:], 0.5).then_inc(hdt_done, 1)
                with act.Fori(0, TOK_ITERS) as i:
                    for r in act_rounds:
                        for g in range(GROUPS):
                            h0 = i * (GROUPS * GH) + g * GH
                            act.wait_ge(pe_round[g], i * ROUNDS + r + 1)
                            if r == R_OUT:
                                act.wait_ge(out_done[g], i * 16)
                                nc.scalar.copy(oo[:, g], ps_s[g][:, :, 0:VCOLS]).then_inc(act_round[g], 1)
                                act.wait_ge(act_round[g], i * ACT_N + ACT_N)
                                act.dma_start(d_h1[:, bass.ds(h0, GH), :], oo[:, g]).then_inc(out_done[g], 16)
                                continue
                            if r == R_DAT:
                                nc.scalar.activation(
                                    uu[:, g, :, 0:TOK_C],
                                    c_all[:, bass.ds(h0 * TOK_C, GH * TOK_C)].rearrange("p (h c) -> p h c", c=TOK_C),
                                    ACT.Copy, scale=sgn_c[:])
                            nc.scalar.copy(pwt[:, g], ps_t[g][:]).then_inc(act_round[g], 1)


D = 512
KD = D // P
SLOTS = 168
SEQ_TOK, SEQ_TXT = 64, 128
SEQ = SEQ_TOK + SEQ_TXT
BATCH = 16
D_IN = 1024
MI = D_IN // P
NH, HP, NS = 16, 64, 64
TAPS = 4
PAD = TAPS - 1
COL_Z, COL_X, COL_B = 0, D_IN, 2 * D_IN
COL_DT, COL_C = COL_B + NS, COL_B + NS + NH
PROJ = COL_C + NS
TB, TC = MI, MI + 1
EPS = 1e-5
E, TOPK, PRIM = 32, 8, 4
SEC = TOPK - PRIM
TOKENS = BATCH * SEQ
ROWS = TOKENS + P
XW = D + E
EXP_TILES = TOKENS // P
SLOT_COLS = E * EXP_TILES + 1
PAIRS = BATCH // 2


def row_chunks(n, size):
    return [(a, min(size, n - a)) for a in range(0, n, size)]


def build_table(nc, win, d_win, d_cat, d_ptab, d_ztab):
    parts = row_chunks(SLOTS, P)
    chunks = row_chunks(PROJ, D)
    with ExitStack() as ctx:
        s = Scope(nc, ctx, "tab")
        cat = s.sb("cat", [P, 2, D])
        ex = s.sb("ex", [P, 2, D])
        xn = s.sb("xn", [P, 2, D])
        xnt = s.sb("xnt", [P, KD, SLOTS])
        zt = s.sb("zt", [P, 2, PROJ])
        nmx = s.sb("nmx", [P, 2])
        sm = s.sb("sm", [P, 2])
        rs = s.sb("rs", [P, 2])
        st = s.sb("st", [P, 2, 6])
        mv = s.sb("mv", [P, 2, 2])
        ve = s.sb("ve", [P, 2])
        rstd = s.sb("rstd", [P, 2])
        mhalf = s.sb("mhalf", [P, 2])
        ident = s.sb("ident", [P, P])
        ps_t = s.bank("ps_t", [P, KD, P])
        ps_t2 = s.bank("ps_t2", [P, KD, P])
        ps_z = [s.bank(f"ps_z{n}", [P, D]) for n in range(4)]
        cat_in = s.sem("cat_in")
        win_in = s.sem("win_in")
        consts = s.sem("consts")
        nmx_done = s.sem("nmx_done")
        ex_done = s.sem("ex_done")
        ve_done = s.sem("ve_done")
        rstd_done = s.sem("rstd_done")
        xn_done = s.sem("xn_done")
        probs_done = s.sem("probs_done")
        t_done = s.sem("t_done")
        xnt_done = s.sem("xnt_done")
        z_done = s.sem("z_done")
        z_read = s.sem("z_read")
        stored = s.sem("stored")
        dve_own = s.sem("dve_own")

        with nc.Block() as block:
            @block.sync
            def _(sp):
                for n, (a, k) in enumerate(parts):
                    sp.dma_start(cat[0:k, n], d_cat[a:a + k, :]).then_inc(cat_in, 16)
                sp.dma_start(win[:], d_win.rearrange("(k p) n -> p k n", p=P)).then_inc(win_in, 16)
                for n, (a, k) in enumerate(parts):
                    sp.wait_ge(probs_done, n + 1)
                    sp.dma_start(d_ptab[a:a + k, :], ex[0:k, n]).then_inc(stored, 16)
                for n, (a, k) in enumerate(parts):
                    sp.wait_ge(z_read, (n + 1) * len(chunks))
                    sp.dma_start(d_ztab[a:a + k, :], zt[0:k, n]).then_inc(stored, 16)
                sp.wait_ge(stored, 64)

            @block.gpsimd
            def _(pool):
                nc.gpsimd.memset(ident[:], 0.0).then_inc(consts, 1)
                nc.gpsimd.memset(mhalf[:], -0.5).then_inc(consts, 1)
                pool.wait_ge(consts, 2)
                nc.gpsimd.affine_select(out=ident[:], in_=ident[:], compare_op=ALU.not_equal, fill=1.0,
                                        base=0, pattern=[[-1, P]], channel_multiplier=1).then_inc(consts, 1)
                for n, (a, k) in enumerate(parts):
                    pool.wait_ge(ve_done, n + 1)
                    nc.gpsimd.tensor_tensor(rstd[0:k, n:n + 1], ve[0:k, n:n + 1], mhalf[0:k, n:n + 1],
                                            ALU.pow).then_inc(rstd_done, 1)

            @block.scalar
            def _(act):
                for n, (a, k) in enumerate(parts):
                    act.wait_ge(nmx_done, n + 1)
                    nc.scalar.activation(ex[0:k, n], cat[0:k, n], ACT.Exp, bias=nmx[0:k, n:n + 1],
                                         accum_out=sm[0:k, n:n + 1]).then_inc(ex_done, 1)
                for n, (a, k) in enumerate(parts):
                    act.wait_ge(t_done, n + 1)
                    nc.scalar.copy(xnt[:, :, a:a + k], (ps_t, ps_t2)[n][:, :, 0:k]).then_inc(xnt_done, 1)

            @block.vector
            def _(dve):
                own = Chain(dve, dve_own)
                for n, (a, k) in enumerate(parts):
                    dve.wait_ge(cat_in, 32)
                    nc.vector.tensor_reduce(nmx[0:k, n:n + 1], cat[0:k, n], AX.X, ALU.max, negate=True).then_inc(nmx_done, 1)
                for n, (a, k) in enumerate(parts):
                    dve.wait_ge(ex_done, n + 1)
                    own.step(nc.vector.reciprocal(rs[0:k, n:n + 1], sm[0:k, n:n + 1]))
                    nc.vector.tensor_scalar(ex[0:k, n], ex[0:k, n], rs[0:k, n:n + 1], None, ALU.mult).then_inc(probs_done, 1)
                    dve.wait_ge(probs_done, n + 1)
                    own.step(nc.vector.bn_stats(st[0:k, n], ex[0:k, n]))
                    own.step(nc.vector.bn_aggr(mv[0:k, n], st[0:k, n]))
                    nc.vector.tensor_scalar(ve[0:k, n:n + 1], mv[0:k, n, 1:2], EPS, None, ALU.add).then_inc(ve_done, 1)
                    dve.wait_ge(rstd_done, n + 1)
                    nc.vector.tensor_scalar(xn[0:k, n], ex[0:k, n], mv[0:k, n, 0:1], rstd[0:k, n:n + 1],
                                            ALU.subtract, ALU.mult).then_inc(xn_done, 1)
                u = 0
                for n, (a, k) in enumerate(parts):
                    for c, w in chunks:
                        u += 1
                        dve.wait_ge(z_done, u)
                        nc.vector.tensor_copy(zt[0:k, n, c:c + w], ps_z[(u - 1) % 4][0:k, 0:w]).then_inc(z_read, 1)

            @block.tensor
            def _(pe):
                pe.wait_ge(consts, 3)
                for n, (a, k) in enumerate(parts):
                    pe.wait_ge(xn_done, n + 1)
                    for t in range(KD):
                        last = nc.tensor.transpose((ps_t, ps_t2)[n][:, t, 0:k], xn[0:k, n, t * P:(t + 1) * P], ident[0:k, 0:k])
                    last.then_inc(t_done, 1)
                pe.wait_ge(win_in, 16)
                u = 0
                for n, (a, k) in enumerate(parts):
                    pe.wait_ge(xnt_done, n + 1)
                    for c, w in chunks:
                        if u >= 4:
                            pe.wait_ge(z_read, u - 3)
                        for t in range(KD):
                            last = nc.tensor.matmul(ps_z[u % 4][0:k, 0:w], xnt[:, t, a:a + k], win[:, t, c:c + w],
                                                    start=t == 0, stop=t == KD - 1)
                        last.then_inc(z_done, 1)
                        u += 1


RING = 3
PROJ_TILES = ([(COL_B, NS + NH, TB), (COL_C, NS, TC)] + [(COL_X + m * P, P, m) for m in range(MI)]
              + [(COL_Z + m * P, P, m) for m in range(MI)])
CONV_TILES = [TB, TC] + list(range(MI))
N_PROJ, N_CONV = len(PROJ_TILES), len(CONV_TILES)
N_XT = 2 * 2 * 2
N_Y = 2 * MI // 2
N_WO = 3
USES_DVE = N_XT + N_Y + N_WO
USES = N_PROJ + USES_DVE
Q_ROWS, Q_EXP, Q_ONE_HOTS, Q_SIM = (3, 4, 5), 7, 13, 15
EARLY = 6
S0 = P
S1 = SEQ - S0


def build_layer(nc, win, macc, a):
    with ExitStack() as ctx:
        s = Scope(nc, ctx, "lay")
        wout = s.sb("wout", [P, MI, D])
        nw = s.sb("nw", [P, MI])
        gate = s.sb("gate", [P, KD, E])
        sim4 = s.sb("sim4", [P, P])
        cw = s.sb("cw", [P, N_CONV, TAPS])
        cb = s.sb("cb", [P, N_CONV])
        dcol = s.sb("dcol", [P, MI])
        dtb = s.sb("dtb", [NH, 1])
        ea = s.sb("ea", [NH, 1])
        txt = s.sb("txt", [P, BATCH], I32)
        txt_p = s.sb("txt_p", [P, 2], I32)
        txt_z = s.sb("txt_z", [P, 2], I32)
        txt_n = s.sb("txt_n", [P, 2], I32)
        zero_i = s.sb("zero_i", [P, 2], I32)
        hin = s.sb("hin", [P, D])
        mv1 = s.sb("mv1", [P, 2])
        ve1 = s.sb("ve1", [P, 1])
        rstd1 = s.sb("rstd1", [P, 1])
        hres = s.sb("hres", [P, 3, D])
        zt = s.sb("zt", [P, 2, PROJ])
        st = s.sb("st", [P, 6])
        mv = s.sb("mv", [P, 3, 2])
        ve = s.sb("ve", [P, 3])
        rstd = s.sb("rstd", [P, 3])
        mhalf = s.sb("mhalf", [P, 3])
        xn = s.sb("xn", [P, D])
        xnt = s.sb("xnt", [P, KD, P])
        zs = s.sb("zs", [P, MI, 2, SEQ])
        xr = s.sb("xr", [P, N_CONV, 2, PAD + SEQ])
        xa = s.sb("xa", [P, N_CONV, 2, SEQ])
        yb = s.sb("yb", [P, MI, 2 * SEQ])
        dtr = s.sb("dtr", [NH, 2, SEQ])
        dtn = s.sb("dtn", [NH, 2, SEQ])
        ones = s.sb("ones", [P, SEQ])
        td_in = s.sb("td_in", [48, 2, SEQ])
        td = s.sb("td", [P, 2, 2, 48])
        m0 = s.sb("m0", [P, 2, NH, SEQ])
        m1 = s.sb("m1", [S1, 2, NH, S1])
        gm = s.sb("gm", [P, 2, SEQ + S1])
        mask = s.sb("mask", [P, SEQ])
        xdt = s.sb("xdt", [P, 2, 2, D_IN])
        ident = s.sb("ident", [P, P])
        lower = s.sb("lower", [P, P], BF16)
        ones_b = s.sb("ones_b", [P, P], BF16)
        ssv = s.sb("ssv", [P, 3])
        rr = s.sb("rr", [P, 3])
        ss_row = s.sb("ss_row", [1, 3 * P])
        x2 = s.sb("x2", [P, 3, XW])
        ybf = yb[:].rearrange("p m t -> p (m t)")
        x2t = ybf[:, 768:1792].rearrange("p (n k t) -> p n k t", n=2, k=KD)
        oht = ybf[:, 1792:2176].rearrange("p (j t) -> p j t", j=3)
        simr = ybf[:, 2176:2560].rearrange("p (j k e) -> p j k e", j=3, k=SEC)
        prod = ybf[:, 0:3 * TOPK * E]
        iota_e = s.sb("iota_e", [P, E])
        lg = s.sb("lg", [P, 3, E])
        mx = s.sb("mx", [P, 3])
        sm = s.sb("sm", [P, 3])
        top = s.sb("top", [P, 3, TOPK])
        topi = s.sb("topi", [P, 3, TOPK], U32)
        topf = s.sb("topf", [P, 3, TOPK])
        wts = s.sb("wts", [P, 3, TOPK])
        oh = s.sb("oh", [P, 3, TOPK, E])
        sims = s.sb("sims", [P, 3, SEC, PRIM])
        best = s.sb("best", [P, 3, SEC])
        take = s.sb("take", [P, 3, SEC, PRIM])
        rem = s.sb("rem", [P, 3, SEC])
        on = s.sb("on", [P, 3, TOPK])
        moved = s.sb("moved", [P, 3, PRIM])
        mk = s.sb("mk", [P, 3, E], BF16)
        pos = s.sb("pos", [P, 3, E])
        posk = s.sb("posk", [P, 3, TOPK])
        posi = s.sb("posi", [P, 3, TOPK], I32)
        hif = s.sb("hif", [P, 3, TOPK])
        slotf = s.sb("slotf", [P, 3, TOPK])
        slot = s.sb("slot", [P, 3, TOPK], I32)
        tokf = s.sb("tokf", [P, 3])
        toki = s.sb("toki", [P, 3], I32)
        dummy = m0[:].rearrange("p b h t -> p (b h t)")[:, 0:SLOT_COLS].bitcast(I32)
        zero = zt[:, 0, 0:XW]

        ring = [s.bank(f"ring{n}", [P, D]) for n in range(RING)]
        ps_tr = s.bank("ps_tr", [P, KD, P])
        ps_g = s.bank("ps_g", [P, 2, SEQ + S1])
        ps_c = s.bank("ps_c", [P, D])
        ps_q = s.bank("ps_q", [P, 3, P])
        ps_pos = s.bank("ps_pos", [P, 3, E])

        par_in = s.sem("par_in")
        c_own = s.sem("c_own")
        consts = s.sem("consts")
        filled = s.sem("filled")
        w_done = s.sem("w_done")
        tok_in = s.sem("tok_in")
        pool_own = s.sem("pool_own")
        gat_z = s.sem("gat_z")
        gat_p = s.sem("gat_p")
        hin_copied = s.sem("hin_copied")
        ve_done = s.sem("ve_done")
        rstd_done = s.sem("rstd_done")
        xn_done = s.sem("xn_done")
        tr_done = s.sem("tr_done")
        xnt_done = s.sem("xnt_done")
        ring_pe = s.sem("ring_pe")
        ring_act = s.sem("ring_act")
        ring_dve = s.sem("ring_dve")
        dtr_done = s.sem("dtr_done")
        nax_done = s.sem("nax_done")
        sp_done = s.sem("sp_done")
        td_in_done = s.sem("td_in_done")
        cum_out = s.sem("cum_out")
        cum_in = s.sem("cum_in")
        td_tr = s.sem("td_tr")
        td_done = s.sem("td_done")
        conv_done = s.sem("conv_done")
        silu_done = s.sem("silu_done")
        g_done = s.sem("g_done")
        gm_done = s.sem("gm_done")
        e_done = s.sem("e_done")
        m_done = s.sem("m_done")
        xdt_done = s.sem("xdt_done")
        y_pe = s.sem("y_pe")
        y_done = s.sem("y_done")
        sq_done = s.sem("sq_done")
        ss_done = s.sem("ss_done")
        row_done = s.sem("row_done")
        cols_done = s.sem("cols_done")
        ssv_done = s.sem("ssv_done")
        rr_done = s.sem("rr_done")
        ve2_done = s.sem("ve2_done")
        rstd2_done = s.sem("rstd2_done")
        x2_done = s.sem("x2_done")
        x2tr_done = s.sem("x2tr_done")
        x2t_done = s.sem("x2t_done")
        lg_pe = s.sem("lg_pe")
        lgs_done = s.sem("lgs_done")
        lge_done = s.sem("lge_done")
        oh_done = s.sem("oh_done")
        oht_pe = s.sem("oht_pe")
        oht_done = s.sem("oht_done")
        sim_pe = s.sem("sim_pe")
        mk_done = s.sem("mk_done")
        pos_pe = s.sem("pos_pe")
        macc_done = s.sem("macc_done")
        slot_done = s.sem("slot_done")
        h_out = s.sem("h_out")
        x2_out = s.sem("x2_out")
        scat = s.sem("scat")
        dve_own = s.sem("dve_own")
        act_own = s.sem("act_own")
        N_PAR = 13

        with nc.Block() as block:
            @block.sync
            def _(sp):
                for dst, src in ((wout[:], a["wout"].rearrange("(m p) n -> p m n", p=P)),
                                 (nw[:], a["nw"]), (gate[:], a["gate"].rearrange("(k p) n -> p k n", p=P)),
                                 (cw[:], a["cw"]), (cb[:], a["cb"]), (dcol[:], a["dcol"]),
                                 (dtb[:], a["dtb"]), (ea[:], a["alog"]), (txt[:], a["txt"])):
                    sp.dma_start(dst, src).then_inc(par_in, 16)
                sp.wait_ge(c_own, 13)
                for j in range(SEC):
                    sp.dma_start(sim4[j * E:(j + 1) * E, j * E:(j + 1) * E], a["sim"]).then_inc(par_in, 16)
                sp.dma_start(a["slots"].rearrange("(p c) o -> p (c o)", p=P), dummy).then_inc(filled, 16)
                sp.dma_start(a["xg"][TOKENS:ROWS, :], zero).then_inc(filled, 16)
                sp.dma_start(a["out"][TOKENS:ROWS, :], zero[:, 0:D]).then_inc(filled, 16)
                sp.wait_ge(filled, 48)

                def load_tokens(i):
                    src = bass.AP(a["h1"].tensor, i * (2 * TOK_H * VCOLS),
                                  [[VCOLS, P], [TOK_C * TOK_H * VCOLS, UROWS], [1, VCOLS]])
                    sp.dma_start(hin[:].rearrange("p (i j) -> p i j", j=VCOLS), src).then_inc(tok_in, 16)

                def store_rows(k):
                    sp.wait_ge(x2_done, k * 3 + 3)
                    for b in range(2):
                        sp.dma_start(a["out"][bass.ds(k * (2 * SEQ) + b * SEQ, SEQ_TOK), :],
                                     hres[b * SEQ_TOK:(b + 1) * SEQ_TOK, 0]).then_inc(h_out, 16)
                        sp.dma_start(a["out"][bass.ds(k * (2 * SEQ) + b * SEQ + SEQ_TOK, SEQ_TXT), :],
                                     hres[:, 1 + b]).then_inc(h_out, 16)

                def store_routed(k):
                    sp.wait_ge(mk_done, k + 1)
                    for b in range(2):
                        sp.dma_start(a["xg"][bass.ds(k * (2 * SEQ) + b * SEQ, SEQ_TOK), :],
                                     x2[b * SEQ_TOK:(b + 1) * SEQ_TOK, 0]).then_inc(x2_out, 16)
                        sp.dma_start(a["xg"][bass.ds(k * (2 * SEQ) + b * SEQ + SEQ_TOK, SEQ_TXT), :],
                                     x2[:, 1 + b]).then_inc(x2_out, 16)

                def pair(i, first=False, last=False):
                    if not first:
                        store_rows(i - 1)
                    sp.wait_ge(td_in_done, i + 1)
                    sp.dma_start(a["cum"].rearrange("b h t -> h b t"), td_in[0:NH]).then_inc(cum_out, 16)
                    sp.wait_ge(cum_out, i * 16 + 16)
                    for b in range(2):
                        sp.dma_start(m0[:, b], a["cum"][b:b + 1].rearrange("b h t -> b (h t)").to_broadcast([P, NH * SEQ]).rearrange("p (h t) -> p h t", h=NH)).then_inc(cum_in, 16)
                        sp.dma_start(m1[:, b], a["cum"][b:b + 1, :, S0:SEQ].to_broadcast([S1, NH, S1])).then_inc(cum_in, 16)
                    if not first:
                        store_routed(i - 1)
                    if not last:
                        sp.wait_ge(xn_done, i + 1)
                        sp.wait_ge(hin_copied, i + 1)
                        load_tokens(i + 1)

                load_tokens(0)
                pair(0, first=True)
                with sp.Fori(1, PAIRS - 1) as i:
                    pair(i)
                pair(PAIRS - 1, last=True)
                store_rows(PAIRS - 1)
                store_routed(PAIRS - 1)
                sp.wait_ge(h_out, PAIRS * 64)
                sp.wait_ge(x2_out, PAIRS * 64)

            @block.gpsimd
            def _(pool):
                c = Chain(pool, c_own)
                c.step(nc.gpsimd.memset(ident[:], 0.0))
                c.step(nc.gpsimd.affine_select(out=ident[:], in_=ident[:], compare_op=ALU.not_equal, fill=1.0,
                                               base=0, pattern=[[-1, P]], channel_multiplier=1))
                c.step(nc.gpsimd.memset(mask[:], 1.0))
                c.step(nc.gpsimd.affine_select(out=mask[:], in_=mask[:], compare_op=ALU.is_ge, fill=0.0,
                                               base=0, pattern=[[1, SEQ]], channel_multiplier=-1))
                c.step(nc.gpsimd.memset(lower[:], 1.0))
                c.step(nc.gpsimd.affine_select(out=lower[:], in_=lower[:], compare_op=ALU.is_gt, fill=0.0,
                                               base=0, pattern=[[1, P]], channel_multiplier=-1))
                c.step(nc.gpsimd.memset(ones_b[:], 1.0))
                c.step(nc.gpsimd.memset(zero, 0.0))
                c.step(nc.gpsimd.memset(mhalf[:], -0.5))
                c.step(nc.gpsimd.memset(sim4[:], 0.0))
                c.step(nc.gpsimd.memset(td_in[:], 0.0))
                c.step(nc.gpsimd.memset(xr[:, :, :, 0:PAD], 0.0))
                c.step(nc.gpsimd.iota(dummy, pattern=[[0, SLOT_COLS]], base=TOKENS, channel_multiplier=1))
                c.step(nc.gpsimd.memset(zero_i[:], 0))
                c.step(nc.gpsimd.memset(ones[:], 1.0))
                c.step(nc.gpsimd.memset(macc[:], 0.0))
                c.step(nc.gpsimd.iota(iota_e[:], pattern=[[1, E]], base=0, channel_multiplier=0,
                                      allow_small_or_imprecise_dtypes=True))
                c.step(nc.gpsimd.iota(tokf[0:SEQ_TOK, 0:1], pattern=[[0, 1]], base=0, channel_multiplier=1,
                                      allow_small_or_imprecise_dtypes=True))
                c.step(nc.gpsimd.iota(tokf[SEQ_TOK:P, 0:1], pattern=[[0, 1]], base=SEQ, channel_multiplier=1,
                                      allow_small_or_imprecise_dtypes=True))
                c.step(nc.gpsimd.iota(tokf[:, 1:3], pattern=[[SEQ, 2]], base=SEQ_TOK, channel_multiplier=1,
                                      allow_small_or_imprecise_dtypes=True))
                pool.wait_ge(par_in, N_PAR * 16)
                nc.gpsimd.affine_select(out=sim4[:], in_=sim4[:], compare_op=ALU.not_equal, fill=1.0,
                                        base=0, pattern=[[-1, P]], channel_multiplier=1).then_inc(consts, 1)
                pool.wait_ge(filled, 48)
                own = Chain(pool, pool_own)

                def gather_rows(dst, table, index, b, sem):
                    off = bass.IndirectOffsetOnAxis(ap=index[:, b:b + 1], axis=0)
                    pool.indirect_dma_start(out=dst, out_offset=None, in_=a[table], in_offset=off,
                                            bounds_check=SLOTS - 1).then_inc(sem, 16)

                def next_tokens(i):
                    own.step(nc.gpsimd.tensor_copy(txt_n[:], txt[:, bass.ds(i * 2, 2)]))
                    wait_before(pool, ring_pe, i * USES - USES_DVE)
                    own.step(nc.gpsimd.tensor_tensor(txt_z[:], txt_n[:], zero_i[:], ALU.add))
                    for b in range(2):
                        gather_rows(zt[:, b], "ztab", txt_z, b, gat_z)
                    pool.wait_ge(ve_done, i + 1)
                    nc.gpsimd.tensor_tensor(rstd1[:], ve1[:], mhalf[:, 0:1], ALU.pow).then_inc(rstd_done, 1)

                def fill_lists(k):
                    pool.wait_ge(slot_done, k + 1)
                    own.step(nc.gpsimd.tensor_tensor(slotf[:], posk[:], on[:], ALU.add))
                    own.step(nc.gpsimd.tensor_copy(slot[:], slotf[:]))
                    for j in range(3):
                        for c in range(TOPK):
                            pool.indirect_dma_start(
                                out=a["slots"], out_offset=bass.IndirectOffsetOnAxis(ap=slot[:, j, c:c + 1], axis=0),
                                in_=toki[:, j:j + 1], in_offset=None,
                                bounds_check=P * SLOT_COLS - 1, oob_is_err=False).then_inc(scat, 16)

                def pair(i, first=False, last=False):
                    own.mark(nc.gpsimd.tensor_copy(txt_p[:], txt[:, bass.ds(i * 2, 2)]))
                    wait_before(pool, h_out, i * 64)
                    pool.wait_ge(tok_in, i * 16 + 16)
                    nc.gpsimd.tensor_tensor(hres[:, 0], hin[:], ones[:, 0:1].to_broadcast([P, D]), ALU.mult).then_inc(hin_copied, 1)
                    own.wait()
                    for b in range(2):
                        gather_rows(hres[:, 1 + b], "ptab", txt_p, b, gat_p)
                    if not first:
                        fill_lists(i - 1)
                    if not last:
                        next_tokens(i + 1)
                    pool.wait_ge(ssv_done, i + 1)
                    nc.gpsimd.tensor_tensor(rr[:], ssv[:], mhalf[:], ALU.pow).then_inc(rr_done, 1)
                    pool.wait_ge(ve2_done, i + 1)
                    nc.gpsimd.tensor_tensor(rstd[:], ve[:], mhalf[:], ALU.pow).then_inc(rstd2_done, 1)
                    own.restart()

                next_tokens(0)
                pair(0, first=True)
                with pool.Fori(1, PAIRS - 1) as i:
                    pair(i)
                pair(PAIRS - 1, last=True)
                fill_lists(PAIRS - 1)
                pool.wait_ge(scat, PAIRS * 3 * TOPK * 16)

            @block.scalar
            def _(act):
                act.wait_ge(par_in, N_PAR * 16)
                nc.scalar.activation(ea[:], ea[:], ACT.Exp).then_inc(w_done, 1)
                own = Chain(act, act_own)

                def routed_rows(k, j):
                    act.wait_ge(x2tr_done, k * 3 + j + 1)
                    nc.scalar.copy(x2t[:, j % 2], ps_tr[:]).then_inc(x2t_done, 1)

                def router_exp(k):
                    act.wait_ge(lgs_done, k + 1)
                    nc.scalar.activation(lg[:], lg[:], ACT.Exp).then_inc(lge_done, 1)

                def one_hots(k):
                    act.wait_ge(oht_pe, k + 1)
                    nc.scalar.copy(oht, ps_q[:]).then_inc(oht_done, 1)

                def projected(i, q):
                    act.wait_ge(ring_pe, i * USES + q + 1)
                    return ring[q % RING][:, 0:2 * SEQ].rearrange("p (b t) -> p b t", b=2)

                def z_silu(i, n):
                    nc.scalar.activation(zs[:, n], projected(i, 2 + MI + n), ACT.Silu).then_inc(ring_act, 1)

                def x_silu(i, n):
                    m = CONV_TILES[n]
                    k = P if m < MI else NS
                    act.wait_ge(conv_done, i * N_CONV + n + 1)
                    nc.scalar.activation(xa[0:k, m], xa[0:k, m], ACT.Silu).then_inc(silu_done, 1)

                def pair(i, first=False):
                    act.wait_ge(tr_done, i + 1)
                    nc.scalar.copy(xnt[:], ps_tr[:]).then_inc(xnt_done, 1)
                    for q in range(2 + MI):
                        _, w, m = PROJ_TILES[q]
                        k = min(w, P) if m < MI else NS
                        bank = projected(i, q)
                        if m == TB:
                            nc.scalar.copy(dtr[:], bank[NS:NS + NH]).then_inc(dtr_done, 1)
                        nc.scalar.copy(xr[0:k, m, :, PAD:PAD + SEQ], bank[0:k])
                        nc.scalar.activation(xa[0:k, m], bank[0:k], ACT.Identity, bias=cb[0:k, m:m + 1],
                                             scale=cw[0:k, m, TAPS - 1:TAPS]).then_inc(ring_act, 1)
                        if q == 3:
                            act.wait_ge(nax_done, i + 1)
                            own.step(nc.scalar.activation(dtn[:], dtn[:], ACT.Exp))
                            nc.scalar.activation(dtn[:], dtn[:], ACT.Ln, bias=1.0).then_inc(sp_done, 1)
                        if not first and q in Q_ROWS:
                            routed_rows(i - 1, Q_ROWS.index(q))
                        if not first and q == Q_EXP:
                            router_exp(i - 1)
                    for n in range(EARLY):
                        z_silu(i, n)
                        if not first and 2 + MI + n == Q_ONE_HOTS:
                            one_hots(i - 1)
                        x_silu(i, n)
                    for n in range(EARLY, MI):
                        z_silu(i, n)
                    act.wait_ge(cum_in, i * 64 + 64)
                    act.wait_ge(td_done, i + 1)
                    for b in range(2):
                        for h in range(NH):
                            nc.scalar.activation(m0[:, b, h], m0[:, b, h], ACT.Exp, bias=td[:, b, 0, h:h + 1], scale=-1.0)
                            last = nc.scalar.activation(m1[:, b, h], m1[:, b, h], ACT.Exp, bias=td[0:S1, b, 1, h:h + 1], scale=-1.0)
                        last.then_inc(e_done, 1)
                    for n in range(EARLY, N_CONV):
                        x_silu(i, n)
                    act.wait_ge(y_done, i * 2 + 2)
                    nc.scalar.activation(xa[:, 0:MI].rearrange("p m b t -> p m (b t)"), yb[:], ACT.Square).then_inc(sq_done, 1)
                    act.wait_ge(ss_done, i + 1)
                    nc.scalar.copy(ss_row[:], ps_c[0:1, 0:3 * P]).then_inc(row_done, 1)
                    own.restart()

                pair(0, first=True)
                with act.Fori(1, PAIRS) as i:
                    pair(i)
                for j in range(3):
                    routed_rows(PAIRS - 1, j)
                router_exp(PAIRS - 1)
                one_hots(PAIRS - 1)

            @block.tensor
            def _(pe):
                mm, tr = nc.tensor.matmul, nc.tensor.transpose
                pe.wait_ge(consts, 1)
                pe.wait_ge(w_done, 2)

                def ring_wait(i, u):
                    v = u - RING
                    if v < 0:
                        if not isinstance(i, int) or i > 0:
                            use = max(w for w in range(USES) if w % RING == u % RING)
                            pe.wait_ge(ring_dve, i * USES_DVE + (use + 1 - USES))
                    elif v < N_PROJ:
                        pe.wait_ge(ring_act, i * N_PROJ + v + 1)
                    else:
                        pe.wait_ge(ring_dve, i * USES_DVE + v - N_PROJ + 1)

                def routed_rows(k, j):
                    pe.wait_ge(x2_done, k * 3 + j + 1)
                    for t in range(KD):
                        last = tr(ps_tr[:, t], x2[:, j, t * P:(t + 1) * P], ident[:])
                    last.then_inc(x2tr_done, 1)

                def router_logits(k, j):
                    if j == 0:
                        pe.wait_ge(ssv_done, k + 1)
                    pe.wait_ge(x2t_done, k * 3 + j + 1)
                    for t in range(KD):
                        last = mm(ps_g[:, 0, j * E:(j + 1) * E], x2t[:, j % 2, t], gate[:, t], start=t == 0, stop=t == KD - 1)
                    last.then_inc(lg_pe, 1)

                def one_hots(k):
                    pe.wait_ge(oh_done, k + 1)
                    for j in range(3):
                        last = tr(ps_q[:, j], oh[:, j, PRIM:TOPK].rearrange("p k e -> p (k e)"), ident[:])
                    last.then_inc(oht_pe, 1)

                def similarities(k):
                    pe.wait_ge(oht_done, k + 1)
                    for j in range(3):
                        last = mm(ps_q[:, j], oht[:, j], sim4[:], start=True, stop=True)
                    last.then_inc(sim_pe, 1)

                def places(k):
                    pe.wait_ge(mk_done, k + 1)
                    for j in range(3):
                        mm(ps_pos[:, j], lower[:], mk[:, j], start=True, stop=False)
                        for q in range(j):
                            mm(ps_pos[:, j], ones_b[:], mk[:, q], start=False, stop=False)
                        last = mm(ps_pos[:, j], ones_b[:], macc[:], start=False, stop=True)
                    last.then_inc(pos_pe, 1)

                def pair(i, first=False):
                    pe.wait_ge(xn_done, i + 1)
                    for t in range(KD):
                        last = tr(ps_tr[:, t], xn[:, t * P:(t + 1) * P], ident[:])
                    last.then_inc(tr_done, 1)
                    pe.wait_ge(xnt_done, i + 1)
                    for q, (col, w, m) in enumerate(PROJ_TILES):
                        ring_wait(i, q)
                        if q == 9:
                            pe.wait_ge(td_in_done, i + 1)
                        bank = ring[q % RING][0:w, 0:2 * SEQ].rearrange("p (b t) -> p b t", b=2)
                        for t in range(KD):
                            mm(bank[:, :, 0:SEQ_TOK], win[:, t, col:col + w],
                               xnt[:, t].rearrange("p (b t) -> p b t", b=2), start=t == 0, stop=t == KD - 1)
                        if q == 0:
                            pe.wait_ge(gat_z, i * 32 + 32)
                        for b in range(2):
                            last = tr(bank[:, b, SEQ_TOK:SEQ], zt[:, b, col:col + w], ident[:])
                        last.then_inc(ring_pe, 1)
                        if q == 9:
                            for b in range(2):
                                tr(ps_tr[:, 0, b * 48:(b + 1) * 48], td_in[:, b, 0:S0], ident[0:48, 0:48])
                                last = tr(ps_tr[0:S1, 1, b * 48:(b + 1) * 48], td_in[:, b, S0:SEQ], ident[0:48, 0:48])
                            last.then_inc(td_tr, 1)
                        if not first and q - 1 in Q_ROWS:
                            router_logits(i - 1, Q_ROWS.index(q - 1))
                        if not first and q in Q_ROWS:
                            routed_rows(i - 1, Q_ROWS.index(q))
                        if not first and q == Q_ONE_HOTS:
                            one_hots(i - 1)
                        if not first and q == Q_SIM:
                            similarities(i - 1)
                    pe.wait_ge(silu_done, i * N_CONV + 2)
                    for b in range(2):
                        mm(ps_g[:, b, 0:SEQ], xa[0:NS, TB, b, 0:S0], xa[0:NS, TC, b], start=True, stop=True)
                        last = mm(ps_g[0:S1, b, SEQ:SEQ + S1], xa[0:NS, TB, b, S0:SEQ], xa[0:NS, TC, b, S0:SEQ], start=True, stop=True)
                    last.then_inc(g_done, 1)
                    u = N_PROJ

                    def x_transposes(half, u):
                        for b in range(2):
                            for part, (t0, n) in enumerate(((0, S0), (S0, S1))):
                                if part == 0:
                                    ring_wait(i, u)
                                    ring_wait(i, u + 1)
                                for m in range(4):
                                    last = tr(ring[u % RING][0:n, m * P:(m + 1) * P], xa[:, half * 4 + m, b, t0:t0 + n], ident[:])
                                last.then_inc(ring_pe, 1)
                                u += 1
                        return u

                    def y_products(b, u):
                        pe.wait_ge(m_done, i * 2 + b + 1)
                        for m2 in range(MI // 2):
                            ring_wait(i, u)
                            for m in (2 * m2, 2 * m2 + 1):
                                c0 = (m % 2) * SEQ
                                for h in (2 * m, 2 * m + 1):
                                    p0 = (h % 2) * HP
                                    mm(ring[u % RING][p0:p0 + HP, c0:c0 + SEQ], xdt[:, b, 0, h * HP:(h + 1) * HP],
                                       m0[:, b, h], start=True, stop=False)
                                    last = mm(ring[u % RING][p0:p0 + HP, c0 + S0:c0 + SEQ], xdt[0:S1, b, 1, h * HP:(h + 1) * HP],
                                              m1[:, b, h], start=False, stop=True)
                            last.then_inc(ring_pe, 1)
                            u += 1
                        return u

                    pe.wait_ge(silu_done, i * N_CONV + EARLY)
                    u = x_transposes(0, u)
                    if not first:
                        places(i - 1)
                    pe.wait_ge(silu_done, i * N_CONV + N_CONV)
                    u = x_transposes(1, u)
                    for b in range(2):
                        u = y_products(b, u)
                    pe.wait_ge(y_done, i * 2 + 2)
                    for j in range(3):
                        ring_wait(i, u)
                        if j == 2:
                            pe.wait_ge(row_done, i + 1)
                            for c in range(3):
                                last = mm(ps_c[:, 3 * P + c:3 * P + c + 1], ss_row[:, c * P:(c + 1) * P], ones[0:1, 0:1], start=True, stop=True)
                            last.then_inc(cols_done, 1)
                        for m in range(MI):
                            last = mm(ring[u % RING][:], yb[:, m, j * P:(j + 1) * P], wout[:, m], start=m == 0, stop=m == MI - 1)
                        last.then_inc(ring_pe, 1)
                        if j == 0:
                            pe.wait_ge(sq_done, i + 1)
                            for m in range(MI):
                                last = mm(ps_c[0:1, 0:3 * P], ones[:, 0:1], xa[:, m].rearrange("p b t -> p (b t)"), start=m == 0, stop=m == MI - 1)
                            last.then_inc(ss_done, 1)
                        u += 1
                    assert u == USES

                pair(0, first=True)
                with pe.Fori(1, PAIRS) as i:
                    pair(i)
                for j in range(3):
                    routed_rows(PAIRS - 1, j)
                    router_logits(PAIRS - 1, j)
                one_hots(PAIRS - 1)
                similarities(PAIRS - 1)
                places(PAIRS - 1)

            @block.vector
            def _(dve):
                v = nc.vector
                own = Chain(dve, dve_own)
                dve.wait_ge(par_in, N_PAR * 16)
                dve.wait_ge(consts, 1)
                v.tensor_tensor(wout[:], wout[:], nw[:].unsqueeze(2).to_broadcast([P, MI, D]), ALU.mult).then_inc(w_done, 1)
                dve.wait_ge(w_done, 2)

                pk = prod.rearrange("p (j k e) -> p (j k) e", k=TOPK, e=E)
                ohk = oh[:].rearrange("p j k e -> p (j k) e")

                def new_tokens(i):
                    dve.wait_ge(tok_in, i * 16 + 16)
                    own.step(v.bn_stats(st[:], hin[:]))
                    own.step(v.bn_aggr(mv1[:], st[:]))
                    v.tensor_scalar(ve1[:], mv1[:, 1:2], EPS, None, ALU.add).then_inc(ve_done, 1)

                def norm_tokens(i):
                    dve.wait_ge(rstd_done, i + 1)
                    wait_before(dve, tr_done, i)
                    v.tensor_scalar(xn[:], hin[:], mv1[:, 0:1], rstd1[:], ALU.subtract, ALU.mult).then_inc(xn_done, 1)

                def routed_rows(k):
                    dve.wait_ge(rstd2_done, k + 1)
                    wait_before(dve, x2_out, k * 64)
                    for j in range(3):
                        v.tensor_scalar(x2[:, j, 0:D], hres[:, j], mv[:, j, 0:1], rstd[:, j:j + 1], ALU.subtract, ALU.mult).then_inc(x2_done, 1)

                def router_choices(k):
                    dve.wait_ge(lg_pe, k * 3 + 3)
                    lgp = ps_g[:, 0, 0:3 * E].rearrange("p (j e) -> p j e", e=E)
                    own.step(v.tensor_reduce(mx[:], lgp, AX.X, ALU.max))
                    v.tensor_tensor(lg[:], lgp, mx[:].unsqueeze(2).to_broadcast([P, 3, E]), ALU.subtract).then_inc(lgs_done, 1)
                    dve.wait_ge(lge_done, k + 1)
                    own.step(v.tensor_reduce(sm[:], lg[:], AX.X, ALU.add))
                    own.step(v.reciprocal(sm[:], sm[:]))
                    own.step(v.tensor_tensor(lg[:], lg[:], sm[:].unsqueeze(2).to_broadcast([P, 3, E]), ALU.mult))
                    for j in range(3):
                        own.step(v.max(top[:, j], lg[:, j]))
                        own.mark(v.max_index(topi[:, j], top[:, j], lg[:, j]))
                    own.step(v.tensor_reduce(sm[:], top[:], AX.X, ALU.add))
                    own.step(v.tensor_copy(topf[:], topi[:]))
                    own.step(v.tensor_scalar(sm[:], sm[:], 1e-12, None, ALU.max))
                    own.step(v.reciprocal(sm[:], sm[:]))
                    own.step(v.tensor_tensor(wts[:], top[:], sm[:].unsqueeze(2).to_broadcast([P, 3, TOPK]), ALU.mult))
                    iot = iota_e[:].unsqueeze(1).to_broadcast([P, 3 * TOPK, E])
                    v.tensor_tensor(oh[:].rearrange("p j k e -> p (j k) e"), iot,
                                    topf[:].rearrange("p j k -> p (j k)").unsqueeze(2).to_broadcast([P, 3 * TOPK, E]),
                                    ALU.is_equal).then_inc(oh_done, 1)
                    dve.wait_ge(oh_done, k + 1)

                def router_weights(k):
                    dve.wait_ge(sim_pe, k + 1)
                    own.step(v.tensor_copy(simr.rearrange("p j k e -> p j (k e)"), ps_q[:]))
                    pr = prod[:, 0:SEC * PRIM * E].rearrange("p (a b e) -> p a b e", a=SEC, b=PRIM)
                    for j in range(3):
                        own.step(v.tensor_tensor(pr, simr[:, j].unsqueeze(2).to_broadcast([P, SEC, PRIM, E]),
                                                 oh[:, j, 0:PRIM].unsqueeze(1).to_broadcast([P, SEC, PRIM, E]), ALU.mult))
                        own.step(v.tensor_reduce(sims[:, j], pr, AX.X, ALU.add))
                    own.step(v.tensor_reduce(best[:], sims[:], AX.X, ALU.max))
                    own.step(v.tensor_tensor(take[:], sims[:], best[:].unsqueeze(3).to_broadcast([P, 3, SEC, PRIM]), ALU.is_equal))
                    own.step(v.tensor_scalar(rem[:], best[:], 0.5, None, ALU.is_ge))
                    own.step(v.tensor_scalar(on[:, :, PRIM:TOPK], rem[:], -1.0, 1.0, ALU.mult, ALU.add))
                    for q in range(PRIM):
                        own.step(v.tensor_tensor(take[:, :, :, q], take[:, :, :, q], rem[:], ALU.mult))
                        own.step(v.tensor_tensor(rem[:], rem[:], take[:, :, :, q], ALU.subtract))
                    own.step(v.tensor_tensor(take[:], take[:], wts[:, :, PRIM:TOPK].unsqueeze(3).to_broadcast([P, 3, SEC, PRIM]), ALU.mult))
                    own.step(v.tensor_reduce(moved[:], take[:].rearrange("p j s q -> p j q s"), AX.X, ALU.add))
                    own.step(v.tensor_tensor(wts[:, :, 0:PRIM], wts[:, :, 0:PRIM], moved[:], ALU.add))
                    own.step(v.tensor_tensor(wts[:, :, PRIM:TOPK], wts[:, :, PRIM:TOPK], on[:, :, PRIM:TOPK], ALU.mult))
                    own.step(v.tensor_scalar(on[:], wts[:], 0.0, None, ALU.is_gt))

                    def per_choice(vals):
                        return vals.rearrange("p j k -> p (j k)").unsqueeze(2).to_broadcast([P, 3 * TOPK, E])

                    own.step(v.tensor_tensor(pk, ohk, per_choice(wts[:]), ALU.mult))
                    own.step(v.tensor_reduce(x2[:, :, D:XW], prod.rearrange("p (j k e) -> p j e k", k=TOPK, e=E), AX.X, ALU.add))
                    v.tensor_scalar(mk[:], x2[:, :, D:XW], 0.0, None, ALU.is_gt).then_inc(mk_done, 1)

                def router_places(k):
                    dve.wait_ge(pos_pe, k + 1)
                    dve.wait_ge(mk_done, k + 1)
                    own.step(v.tensor_copy(pos[:], ps_pos[:]))
                    for j in range(3):
                        own.step(v.tensor_tensor(macc[:], macc[:], mk[:, j], ALU.add))
                    for j in range(3):
                        own.step(v.tensor_tensor(pk[:, j * TOPK:(j + 1) * TOPK], oh[:, j], pos[:, j].unsqueeze(1).to_broadcast([P, TOPK, E]), ALU.mult))
                    own.step(v.tensor_reduce(posk[:].rearrange("p j k -> p (j k)"), pk, AX.X, ALU.add))
                    wait_before(dve, scat, k * (3 * TOPK * 16))
                    own.step(v.tensor_copy(posi[:], posk[:]))
                    own.step(v.tensor_scalar(posi[:], posi[:], 7, None, ALU.arith_shift_right))
                    own.step(v.tensor_copy(hif[:], posi[:]))
                    own.step(v.tensor_scalar(posk[:], posk[:], float(SLOT_COLS), None, ALU.mult))
                    own.step(v.scalar_tensor_tensor(posk[:], hif[:], -float(P * SLOT_COLS - 1), posk[:], ALU.mult, ALU.add))
                    own.step(v.scalar_tensor_tensor(posk[:], topf[:], float(EXP_TILES), posk[:], ALU.mult, ALU.add))
                    own.mark(v.tensor_copy(toki[:], tokf[:]))
                    v.tensor_scalar(on[:], on[:], -1.0e6, 1.0e6, ALU.mult, ALU.add).then_inc(slot_done, 1)
                    own.step(v.tensor_scalar(tokf[:], tokf[:], float(2 * SEQ), None, ALU.add))

                def pair(i, first=False, last=False):
                    if not first:
                        routed_rows(i - 1)
                    dve.wait_ge(dtr_done, i + 1)
                    own.step(v.tensor_scalar(dtr[:], dtr[:], dtb[:], None, ALU.add))
                    own.step(v.tensor_scalar(dtn[:], dtr[:], -1.0, None, ALU.mult))
                    v.tensor_tensor(dtn[:], dtn[:], dtr[:], ALU.min).then_inc(nax_done, 1)
                    dve.wait_ge(nax_done, i + 1)

                    def conv(n0):
                        for k in reversed(range(TAPS - 1)):
                            for n in (n0, n0 + 1):
                                m = CONV_TILES[n]
                                r = P if m < MI else NS
                                src = xr[0:r, m, :, k:k + SEQ]
                                if k < TAPS - 2:
                                    own.wait(own.n if (k, n) == (0, n0 + 1) else own.n - 1)
                                ins = v.scalar_tensor_tensor(xa[0:r, m], src, cw[0:r, m, k:k + 1], xa[0:r, m], ALU.mult, ALU.add)
                                if k == 0:
                                    ins.then_inc(conv_done, 1)
                                else:
                                    own.mark(ins)

                    dve.wait_ge(ring_act, i * N_PROJ + 2)
                    conv(0)
                    dve.wait_ge(sp_done, i + 1)
                    own.step(v.scalar_tensor_tensor(td_in[32:48], dtr[:], 0.0, dtn[:], ALU.max, ALU.add))
                    own.step(v.tensor_scalar(dtr[:], td_in[32:48], ea[:], None, ALU.mult))
                    for b in range(2):
                        step = v.tensor_tensor_scan(td_in[0:NH, b], ones[0:NH], dtr[:, b], 0.0, ALU.mult, ALU.add)
                    step.then_inc(td_in_done, 1)
                    if not first:
                        router_choices(i - 1)
                    for n in range(2, EARLY, 2):
                        dve.wait_ge(ring_act, i * N_PROJ + n + 2)
                        conv(n)
                    dve.wait_ge(td_tr, i + 1)
                    v.tensor_copy(td[:, :, 0], ps_tr[:, 0, 0:96].rearrange("p (b c) -> p b c", b=2))
                    v.tensor_copy(td[0:S1, :, 1], ps_tr[0:S1, 1, 0:96].rearrange("p (b c) -> p b c", b=2)).then_inc(td_done, 1)
                    if not first:
                        router_weights(i - 1)
                    dve.wait_ge(g_done, i + 1)
                    v.tensor_tensor(gm[:, :, 0:SEQ], ps_g[:, :, 0:SEQ], mask[:].unsqueeze(1).to_broadcast([P, 2, SEQ]), ALU.mult)
                    v.tensor_tensor(gm[0:S1, :, SEQ:SEQ + S1], ps_g[0:S1, :, SEQ:SEQ + S1],
                                    mask[0:S1, 0:S1].unsqueeze(1).to_broadcast([S1, 2, S1]), ALU.mult).then_inc(gm_done, 1)

                    def x_dt(half, u):
                        for b in range(2):
                            for part, n in enumerate((S0, S1)):
                                dve.wait_ge(ring_pe, i * USES + u + 1)
                                dts = td[0:n, b, part, 32 + half * 8:40 + half * 8].unsqueeze(2).to_broadcast([n, 8, HP])
                                v.tensor_tensor(xdt[0:n, b, part, half * 512:(half + 1) * 512].rearrange("p (h c) -> p h c", c=HP),
                                                ring[u % RING][0:n].rearrange("p (h c) -> p h c", c=HP), dts, ALU.mult).then_inc(ring_dve, 1)
                                u += 1
                        return u

                    dve.wait_ge(td_done, i + 1)
                    u = x_dt(0, N_PROJ)
                    for n in range(EARLY, N_CONV, 2):
                        dve.wait_ge(ring_act, i * N_PROJ + n + 2)
                        conv(n)
                    dve.wait_ge(gm_done, i + 1)
                    for b in range(2):
                        dve.wait_ge(e_done, i * 2 + b + 1)
                        v.scalar_tensor_tensor(m0[:, b], m0[:, b], 1.0, gm[:, b, 0:SEQ].unsqueeze(1).to_broadcast([P, NH, SEQ]),
                                               ALU.min, ALU.mult)
                        v.scalar_tensor_tensor(m1[:, b], m1[:, b], 1.0, gm[0:S1, b, SEQ:SEQ + S1].unsqueeze(1).to_broadcast([S1, NH, S1]),
                                               ALU.min, ALU.mult).then_inc(m_done, 1)
                        if b == 0:
                            u = x_dt(1, u)
                    if not first:
                        router_places(i - 1)
                    if not last:
                        new_tokens(i + 1)
                    for b in range(2):
                        for m2 in range(MI // 2):
                            dve.wait_ge(ring_pe, i * USES + u + 1)
                            for m in (2 * m2, 2 * m2 + 1):
                                c0 = (m % 2) * SEQ
                                step = v.scalar_tensor_tensor(xr[:, m, b, PAD:PAD + SEQ], xa[:, m, b], dcol[:, m:m + 1],
                                                              ring[u % RING][:, c0:c0 + SEQ], ALU.mult, ALU.add)
                            step.then_inc(ring_dve, 1)
                            u += 1
                        dve.wait_ge(ring_dve, i * USES_DVE + u - N_PROJ)
                        v.tensor_tensor(yb[:, :, b * SEQ_TOK:(b + 1) * SEQ_TOK], xr[:, 0:MI, b, PAD:PAD + SEQ_TOK],
                                        zs[:, :, b, 0:SEQ_TOK], ALU.mult)
                        v.tensor_tensor(yb[:, :, (1 + b) * P:(2 + b) * P], xr[:, 0:MI, b, PAD + SEQ_TOK:PAD + SEQ],
                                        zs[:, :, b, SEQ_TOK:SEQ], ALU.mult).then_inc(y_done, 1)
                    dve.wait_ge(cols_done, i + 1)
                    v.tensor_scalar(ssv[:], ps_c[:, 3 * P:3 * P + 3], 1.0 / D_IN, EPS, ALU.mult, ALU.add).then_inc(ssv_done, 1)
                    if not last:
                        norm_tokens(i + 1)
                    dve.wait_ge(rr_done, i + 1)
                    dve.wait_ge(gat_p, i * 32 + 32)
                    dve.wait_ge(hin_copied, i + 1)
                    for j in range(3):
                        dve.wait_ge(ring_pe, i * USES + u + 1)
                        v.scalar_tensor_tensor(hres[:, j], ring[u % RING][:], rr[:, j:j + 1], hres[:, j], ALU.mult, ALU.add).then_inc(ring_dve, 1)
                        dve.wait_ge(ring_dve, i * USES_DVE + u - N_PROJ + 1)
                        own.mark(v.bn_stats(st[:], hres[:, j]))
                        own.wait()
                        own.step(v.bn_aggr(mv[:, j], st[:]))
                        u += 1
                    v.tensor_scalar(ve[:], mv[:, :, 1], EPS, None, ALU.add).then_inc(ve2_done, 1)
                    own.restart()

                new_tokens(0)
                norm_tokens(0)
                pair(0, first=True)
                with dve.Fori(1, PAIRS - 1) as i:
                    pair(i)
                pair(PAIRS - 1, last=True)
                routed_rows(PAIRS - 1)
                router_choices(PAIRS - 1)
                router_weights(PAIRS - 1)
                router_places(PAIRS - 1)
                own.restart()


FF = 192
FH = FF // 2
ENTRIES = 256
F_COL, F_W, F_RING, F_CW = range(4)
W_RING = 4
W_DMAS = 2
assert TOKENS * TOPK // P + E + 4 <= ENTRIES


def build_tile_table(nc, macc, tab, thr, iters, d_tab):
    with ExitStack() as ctx:
        s = Scope(nc, ctx, "tbl")
        ones_b = s.sb("ones_b", [P, P], BF16)
        cnt = s.sb("cnt", [P, E])
        cnti = s.sb("cnti", [P, E], I32)
        tiles = s.sb("tiles", [P, E])
        end = s.sb("end", [P, E])
        one = s.sb("one", [P, E])
        gf = s.sb("gf", [P, 2])
        ind = s.sb("ind", [P, 2, E])
        indt = s.sb("indt", [P, 2, E])
        ef = s.sb("ef", [P, 2])
        cs = s.sb("cs", [P, 2])
        neg = s.sb("neg", [P, 2])
        ff = s.sb("ff", [P, 4, 2])
        fi = s.sb("fi", [P, 4, 2], I32)
        thf = s.sb("thf", [1, E])
        itf = s.sb("itf", [1, 1])
        ps = s.bank("ps", [P, E])
        made = s.sem("made")
        counted = s.sem("counted")
        ready = s.sem("ready")
        table_out = s.sem("table_out")
        table_in = s.sem("table_in")
        dve_own = s.sem("dve_own")
        with nc.Block() as block:
            @block.gpsimd
            def _(pool):
                nc.gpsimd.memset(ones_b[:], 1.0).then_inc(made, 1)
                nc.gpsimd.memset(one[:], 1.0).then_inc(made, 1)
                nc.gpsimd.iota(gf[:], pattern=[[P, 2]], base=-1, channel_multiplier=1,
                               allow_small_or_imprecise_dtypes=True).then_inc(made, 1)

            @block.tensor
            def _(pe):
                pe.wait_ge(made, 3)
                nc.tensor.matmul(ps[:], ones_b[:], macc[:], start=True, stop=True).then_inc(counted, 1)

            @block.vector
            def _(dve):
                v = nc.vector
                own = Chain(dve, dve_own)
                dve.wait_ge(made, 3)
                dve.wait_ge(counted, 1)
                own.step(v.tensor_scalar(cnt[:], ps[:], float(P - 1), None, ALU.add))
                own.step(v.tensor_copy(cnti[:], cnt[:]))
                own.step(v.tensor_scalar(cnti[:], cnti[:], 7, None, ALU.arith_shift_right))
                own.step(v.tensor_copy(tiles[:], cnti[:]))
                own.step(v.tensor_tensor_scan(end[:], one[:], tiles[:], 0.0, ALU.mult, ALU.add))
                own.step(v.tensor_tensor(ind[:], end[:].unsqueeze(1).to_broadcast([P, 2, E]),
                                         gf[:].unsqueeze(2).to_broadcast([P, 2, E]), ALU.is_le))
                own.step(v.tensor_reduce(ef[:], ind[:], AX.X, ALU.add))
                own.step(v.tensor_tensor(indt[:], ind[:], tiles[:].unsqueeze(1).to_broadcast([P, 2, E]), ALU.mult))
                own.step(v.tensor_reduce(cs[:], indt[:], AX.X, ALU.add))
                own.step(v.tensor_tensor(cs[:], gf[:], cs[:], ALU.subtract))
                own.step(v.scalar_tensor_tensor(ff[:, F_COL], ef[:], float(EXP_TILES), cs[:], ALU.mult, ALU.add))
                own.step(v.tensor_scalar(neg[:], ff[:, F_COL], 0.0, float(SLOT_COLS), ALU.is_lt, ALU.mult))
                own.step(v.tensor_tensor(ff[:, F_COL], ff[:, F_COL], neg[:], ALU.add))
                own.step(v.tensor_scalar(ff[:, F_COL], ff[:, F_COL], float(SLOT_COLS - 1), None, ALU.min))
                own.step(v.tensor_scalar(ef[:], ef[:], float(E - 1), None, ALU.min))
                own.step(v.tensor_scalar(ff[:, F_W], ef[:], 1.0, float(16 * W_DMAS), ALU.add, ALU.mult))
                own.step(v.tensor_copy(ff[:, F_RING], ef[:]))
                own.step(v.tensor_scalar(ff[:, F_CW], ef[:], float(D), None, ALU.add))
                own.step(v.tensor_copy(fi[:], ff[:]))
                own.step(v.tensor_scalar(fi[:, F_RING], fi[:, F_RING], W_RING - 1, None, ALU.bitwise_and))
                own.step(v.memset(thf[:, 0:W_RING], 0.0))
                own.step(v.tensor_scalar(thf[:, W_RING:E], end[0:1, 0:E - W_RING], 1.0, None, ALU.add))
                own.step(v.tensor_copy(thr[:], thf[:]))
                own.step(v.tensor_scalar(itf[:], end[0:1, E - 1:E], 1.0, None, ALU.add))
                own.step(v.tensor_copy(iters[:], itf[:]))
                v.tensor_scalar(iters[:], iters[:], 1, None, ALU.arith_shift_right).then_inc(ready, 1)
                dve.wait_ge(ready, 1)

            @block.sync
            def _(sp):
                sp.wait_ge(ready, 1)
                with nc.allow_non_contiguous_dma("1024 words of the tile table"):
                    for q in range(4):
                        sp.dma_start(d_tab[q:q + 1, :].rearrange("o (a p) -> p (o a)", p=P), fi[:, q]).then_inc(table_out, 16)
                sp.wait_ge(table_out, 64)
                sp.dma_start(tab[:], d_tab.rearrange("(o q) t -> o q t", o=1)).then_inc(table_in, 16)
                sp.wait_ge(table_in, 16)


def build_experts(nc, tab, thr, iters, a):
    with ExitStack() as ctx:
        s = Scope(nc, ctx, "moe")
        slots = s.sb("slots", [P, SLOT_COLS], I32)
        wgu = s.sb("wgu", [P, W_RING * KD, 2 * FF])
        wd = s.sb("wd", [FH, W_RING * 2, D])
        xg = [s.sb(f"xg{n}", [P, XW]) for n in range(2)]
        xt = [s.sb(f"xt{n}", [P, KD, P]) for n in range(2)]
        sl = [s.sb(f"sl{n}", [P, FF]) for n in range(2)]
        hh = [s.sb(f"hh{n}", [P, FF]) for n in range(2)]
        ht = s.sb("ht", [FH, 2, P])
        yy = [s.sb(f"yy{n}", [P, D]) for n in range(2)]
        idx_g = [s.sb(f"idx_g{n}", [P, 1], I32) for n in range(2)]
        idx_t = s.sb("idx_t", [P, 1], I32)
        zero_i = s.sb("zero_i", [P, 1], I32)
        idx_s = [s.sb(f"idx_s{n}", [P, 1], I32) for n in range(2)]
        ident = s.sb("ident", [P, P])
        ps_gu = [s.bank(f"ps_gu{n}", [P, 2 * FF]) for n in range(2)]
        ps_xt = s.bank("ps_xt", [P, KD, P])
        ps_y = s.bank("ps_y", [P, D])
        ps_ht = s.bank("ps_ht", [P, 2, P])

        slots_in = s.sem("slots_in")
        w_in = s.sem("w_in")
        made = s.sem("made")
        gathered = [s.sem(f"gathered{n}") for n in range(2)]
        added = [s.sem(f"added{n}") for n in range(2)]
        idx_own = s.sem("idx_own")
        t_pe = s.sem("t_pe")
        up_pe = s.sem("up_pe")
        down_pe = s.sem("down_pe")
        ht_pe = s.sem("ht_pe")
        xt_act = s.sem("xt_act")
        sl_act = s.sem("sl_act")
        h_dve = s.sem("h_dve")
        y_dve = s.sem("y_dve")
        ht_dve = s.sem("ht_dve")

        def entry(eng, field, t, hi):
            return eng.value_load(tab[0:1, field, bass.ds(t, 1)], min_val=0, max_val=hi)

        with nc.Block() as block:
            @block.sync
            def _(sp):
                sp.dma_start(slots[:], a["slots"].rearrange("(p c) o -> p (c o)", p=P)).then_inc(slots_in, 16)
                for r in range(W_RING):
                    if r:
                        sp.wait_ge(w_in, 16 * W_DMAS * r)
                    sp.dma_start(wgu[:, r * KD:(r + 1) * KD], a["wgu"][r]).then_inc(w_in, 16)
                    sp.dma_start(wd[:, r * 2:(r + 1) * 2], a["wd"][r]).then_inc(w_in, 16)
                with sp.Fori(0, E // W_RING - 1) as q:
                    for r in range(W_RING):
                        e = q * W_RING + W_RING + r
                        room = sp.value_load(thr[0:1, bass.ds(e, 1)], min_val=1, max_val=ENTRIES)
                        sp.wait_ge(w_in, e * (16 * W_DMAS))
                        sp.wait_ge(down_pe, room)
                        sp.dma_start(wgu[:, r * KD:(r + 1) * KD], a["wgu"][bass.ds(e, 1)].rearrange("o p k n -> p (o k) n")).then_inc(w_in, 16)
                        sp.dma_start(wd[:, r * 2:(r + 1) * 2], a["wd"][bass.ds(e, 1)].rearrange("o p k n -> p (o k) n")).then_inc(w_in, 16)
                sp.wait_ge(w_in, 16 * W_DMAS * E)

            @block.gpsimd
            def _(pool):
                nc.gpsimd.memset(ident[:], 0.0).then_inc(made, 1)
                pool.wait_ge(made, 1)
                nc.gpsimd.affine_select(out=ident[:], in_=ident[:], compare_op=ALU.not_equal, fill=1.0,
                                        base=0, pattern=[[-1, P]], channel_multiplier=1).then_inc(made, 1)
                nc.gpsimd.memset(zero_i[:], 0).then_inc(made, 1)
                pool.wait_ge(made, 3)
                pool.wait_ge(slots_in, 16)
                own = Chain(pool, idx_own)

                def gather(t, n):
                    col = entry(pool, F_COL, t, SLOT_COLS - 1)
                    own.step(nc.gpsimd.tensor_copy(idx_g[n][:], slots[:, bass.ds(col, 1)]))
                    pool.indirect_dma_start(out=xg[n][:], out_offset=None, in_=a["xg"],
                                            in_offset=bass.IndirectOffsetOnAxis(ap=idx_g[n][:, 0:1], axis=0),
                                            bounds_check=ROWS - 1).then_inc(gathered[n], 16)

                def scatter(t, n, y_count):
                    col = entry(pool, F_COL, t, SLOT_COLS - 1)
                    own.step(nc.gpsimd.tensor_copy(idx_t[:], slots[:, bass.ds(col, 1)]))
                    pool.wait_ge(y_dve, y_count)
                    own.step(nc.gpsimd.tensor_tensor(idx_s[n][:], idx_t[:], zero_i[:], ALU.add))
                    pool.indirect_dma_start(out=a["out"], out_offset=bass.IndirectOffsetOnAxis(ap=idx_s[n][:, 0:1], axis=0),
                                            in_=yy[n][:], in_offset=None, bounds_check=ROWS - 1,
                                            compute_op=ALU.add).then_inc(added[n], 16)

                gather(1, 0)
                gather(2, 1)
                own.restart()
                iters_r = pool.value_load(iters[0:1, 0:1], min_val=1, max_val=ENTRIES // 2 - 2)
                with pool.Fori(0, iters_r) as i:
                    for n in range(2):
                        pool.wait_ge(h_dve, i * 2 + n + 1)
                        gather(i * 2 + n + 3, n)
                        if n == 0:
                            pool.wait_ge(added[1], i * 16)
                        else:
                            pool.wait_ge(added[0], i * 16 + 16)
                        scatter(i * 2 + n, n, i * 2 + n + 1)
                    own.restart()
                pool.wait_ge(added[1], iters_r * 16)
                scatter(iters_r * 2, 0, iters_r * 2 + 1)
                pool.wait_ge(added[0], iters_r * 16 + 16)
                for n in range(2):
                    pool.wait_ge(gathered[n], iters_r * 16 + 16)

            @block.scalar
            def _(act):
                iters_r = act.value_load(iters[0:1, 0:1], min_val=1, max_val=ENTRIES // 2 - 2)
                act.wait_ge(t_pe, 1)
                nc.scalar.copy(xt[0][:], ps_xt[:]).then_inc(xt_act, 1)
                with act.Fori(0, iters_r) as i:
                    for n in range(2):
                        act.wait_ge(up_pe, i * 2 + n + 1)
                        nc.scalar.activation(sl[n][:], ps_gu[n][:, 0:FF], ACT.Silu).then_inc(sl_act, 1)
                        act.wait_ge(t_pe, i * 2 + n + 2)
                        nc.scalar.copy(xt[1 - n][:], ps_xt[:]).then_inc(xt_act, 1)

            @block.vector
            def _(dve):
                v = nc.vector
                iters_r = dve.value_load(iters[0:1, 0:1], min_val=1, max_val=ENTRIES // 2 - 2)
                v.memset(ht[:], 0.0).then_inc(ht_dve, 1)
                with dve.Fori(0, iters_r) as i:
                    for n in range(2):
                        cw = entry(dve, F_CW, i * 2 + n + 1, XW - 1)
                        dve.wait_ge(sl_act, i * 2 + n + 1)
                        v.scalar_tensor_tensor(hh[n][:], sl[n][:], xg[n][:, bass.ds(cw, 1)], ps_gu[n][:, FF:2 * FF],
                                               ALU.mult, ALU.mult).then_inc(h_dve, 1)
                        dve.wait_ge(down_pe, i * 2 + n + 1)
                        dve.wait_ge(added[n], i * 16)
                        v.tensor_copy(yy[n][:], ps_y[:]).then_inc(y_dve, 1)
                        dve.wait_ge(ht_pe, i * 2 + n + 1)
                        v.tensor_copy(ht[:], ps_ht[0:FH]).then_inc(ht_dve, 1)
                dve.wait_ge(down_pe, iters_r * 2 + 1)
                dve.wait_ge(added[0], iters_r * 16)
                v.tensor_copy(yy[0][:], ps_y[:]).then_inc(y_dve, 1)

            @block.tensor
            def _(pe):
                mm, tr = nc.tensor.matmul, nc.tensor.transpose
                iters_r = pe.value_load(iters[0:1, 0:1], min_val=1, max_val=ENTRIES // 2 - 2)
                pe.wait_ge(made, 3)
                pe.wait_ge(gathered[0], 16)
                for t in range(KD):
                    last = tr(ps_xt[:, t], xg[0][:, t * P:(t + 1) * P], ident[:])
                last.then_inc(t_pe, 1)

                def down(t, ht_count):
                    r = entry(pe, F_RING, t, W_RING - 1)
                    pe.wait_ge(ht_dve, ht_count)
                    for q in range(2):
                        last = mm(ps_y[:], ht[:, q], wd[:, bass.ds(r * 2 + q, 1)].rearrange("p o n -> p (o n)"), start=q == 0, stop=q == 1)
                    last.then_inc(down_pe, 1)

                with pe.Fori(0, iters_r) as i:
                    for n in range(2):
                        arrivals = entry(pe, F_W, i * 2 + n + 1, 16 * W_DMAS * E)
                        r = entry(pe, F_RING, i * 2 + n + 1, W_RING - 1)
                        pe.wait_ge(w_in, arrivals)
                        pe.wait_ge(xt_act, i * 2 + n + 1)
                        for t in range(KD):
                            last = mm(ps_gu[n][:], xt[n][:, t], wgu[:, bass.ds(r * KD + t, 1)].rearrange("p o n -> p (o n)"), start=t == 0, stop=t == KD - 1)
                        last.then_inc(up_pe, 1)
                        pe.wait_ge(gathered[1 - n], i * 16 + (32 if n else 16))
                        for t in range(KD):
                            last = tr(ps_xt[:, t], xg[1 - n][:, t * P:(t + 1) * P], ident[:])
                        last.then_inc(t_pe, 1)
                        down(i * 2 + n, i * 2 + n + 1)
                        pe.wait_ge(h_dve, i * 2 + n + 1)
                        for q in range(2):
                            last = tr(ps_ht[0:FH, q], hh[n][:, q * FH:(q + 1) * FH], ident[:])
                        last.then_inc(ht_pe, 1)
                down(iters_r * 2, iters_r * 2 + 1)


INPUTS = ("tok_u", "tok_v", "tok_b", "tok_c", "tok_ldt", "win", "cat", "wout", "nw", "gate", "cw", "cb", "dcol",
          "dtb", "alog", "txt", "sim", "wgu", "wd")


def build(nc, a):
    def scratch(name, shape, dt=FP32):
        a[name] = nc.dram_tensor(f"scratch_{name}", shape, dt, kind="Internal").ap()

    scratch("h1", (UROWS * TOK_C, TOK_H, VCOLS))
    scratch("ptab", (SLOTS, D))
    scratch("ztab", (SLOTS, PROJ))
    scratch("cum", (2, NH, SEQ))
    scratch("xg", (ROWS, XW))
    scratch("slots", (P * SLOT_COLS, 1), I32)
    scratch("tab", (4, ENTRIES), I32)
    build_tokens(nc, a["tok_u"], a["tok_v"], a["tok_b"], a["tok_c"], a["tok_ldt"], a["h1"])
    with nc.sbuf_tensor("macc", [P, E], BF16) as macc:
        with nc.sbuf_tensor("win_sb", [P, KD, PROJ], FP32) as win:
            build_table(nc, win, a["win"], a["cat"], a["ptab"], a["ztab"])
            build_layer(nc, win, macc, a)
        with (nc.sbuf_tensor("tile_tab", [1, 4, ENTRIES], I32) as tab, nc.sbuf_tensor("room", [1, E], I32) as thr,
              nc.sbuf_tensor("iters", [1, 1], I32) as iters):
            build_tile_table(nc, macc, tab, thr, iters, a["tab"])
            build_experts(nc, tab, thr, iters, a)


def kernel(**inputs):
    import numpy as np
    import concourse.bacc as bacc
    from concourse.bass_utils import run_bass_kernel_spmd

    x = {k: np.asarray(v) for k, v in inputs.items()}

    def embedding(re, im):
        m = np.concatenate([np.concatenate([re, im], 2), np.concatenate([im, re], 2)], 1)
        return m.transpose(1, 0, 2)

    re, im = x["L0_tok_A"][..., 0], x["L0_tok_A"][..., 1]
    w_in = x["L0_attn_W_in"]
    bc = 2 * D_IN
    w_in = np.concatenate([w_in[:bc + NS], w_in[bc + 2 * NS:], w_in[bc + NS:bc + 2 * NS]])
    conv_w, conv_b = x["L0_attn_conv_w"], x["L0_attn_conv_b"]
    cw = np.zeros((P, N_CONV, TAPS), np.float32)
    cb = np.zeros((P, N_CONV), np.float32)
    cw[:, :MI] = conv_w[:D_IN].reshape(MI, P, TAPS).transpose(1, 0, 2)
    cb[:, :MI] = conv_b[:D_IN].reshape(MI, P).T
    for m, c0 in ((TB, D_IN), (TC, D_IN + NS)):
        cw[:NS, m] = conv_w[c0:c0 + NS]
        cb[:NS, m] = conv_b[c0:c0 + NS]
    arrays = {
        "tok_u": embedding(re, im),
        "tok_v": embedding(re.transpose(0, 2, 1), im.transpose(0, 2, 1)),
        "tok_b": x["L0_tok_B"].transpose(2, 1, 0).reshape(P, TOK_H),
        "tok_c": x["x"].transpose(3, 2, 1, 0).reshape(P, TOK_H * TOK_C),
        "tok_ldt": np.tile(x["L0_tok_log_dt"].reshape(1, TOK_H), (P, 1)),
        "win": w_in.T,
        "cat": x["L0_txt_catid_time_matrix"],
        "wout": x["L0_attn_W_out"].T,
        "nw": x["L0_attn_norm_w"].reshape(MI, P).T,
        "gate": x["L0_ffn_gate_weight"].T,
        "cw": cw, "cb": cb,
        "dcol": np.repeat(x["L0_attn_D"], HP).reshape(MI, P).T,
        "dtb": x["L0_attn_dt_bias"].reshape(NH, 1),
        "alog": x["L0_attn_A_log"].reshape(NH, 1),
        "txt": x["x_txt"].T,
        "sim": x["L0_ffn_similarity"],
        "wgu": x["L0_ffn_gate_up_proj"].reshape(E, 2 * FF, KD, P).transpose(0, 3, 2, 1),
        "wd": x["L0_ffn_down_proj"].reshape(E, D, 2, FH).transpose(0, 3, 2, 1),
    }
    nc = bacc.Bacc("TRN2", target_bir_lowering=False, num_devices=1)
    fed, aps = {}, {}
    for name in INPUTS:
        v = np.ascontiguousarray(arrays[name])
        fed[f"in_{name}"] = v
        aps[name] = nc.dram_tensor(f"in_{name}", v.shape, mybir.dt.from_np(v.dtype), kind="ExternalInput").ap()
    aps["out"] = nc.dram_tensor("out_h", (ROWS, D), FP32, kind="ExternalOutput").ap()
    build(nc, aps)
    r = run_bass_kernel_spmd(nc, [fed], core_ids=[0])
    return r.results[0]["out_h"][:TOKENS].reshape(BATCH, SEQ, D)
```
